# Optimizing a Trainium2 kernel written in Bass

```python
import numpy as np
import jax
import jax.numpy as jnp

def _softmax(x, axis=-1):
    return jax.nn.softmax(x, axis=axis)

def _gelu(x):
    return jax.nn.gelu(x, approximate=True)

def _silu(x):
    return jax.nn.silu(x)

def _sigmoid(x):
    return jax.nn.sigmoid(x)

def _layernorm(x, axis=-1, eps=1e-05):
    m = jnp.mean(x, axis=axis, keepdims=True)
    v = jnp.var(x, axis=axis, keepdims=True)
    return (x - m) / jnp.sqrt(v + eps)

def _scatter_add(tgt, idx, src, axis=0):
    return tgt.at[idx].add(src)

def _segment_sum(src, seg, n):
    return jax.ops.segment_sum(src, seg, n)
kernel_name = 'mk_adj_preln_d1_adj_r2_e39c36'

def setup_inputs(seed: int=0):
    np.random.seed(seed)
    _w = jnp.asarray

    def _rec_inputs():
        import jax
        import jax.numpy as jnp
        _gk = jax.random.key(seed)
        x = -0.0005207 + 1.001 * jax.random.normal(jax.random.fold_in(_gk, 1), (4096, 128), jnp.float32)
        _w = (1.0 + jnp.arange(4096, dtype=jnp.float32)) ** (-0.5)
        _w = _w / _w.mean()
        _pij = jnp.clip(0.00390625 * _w[:, None] * _w[None, :], 0.0, 1.0)
        _a = jax.random.uniform(jax.random.fold_in(_gk, 2), (4096, 4096)) < _pij
        adj = _a.astype(jnp.int32)
        return (x, adj)
    x, adj = _rec_inputs()

    def _L0_gnn_setup():
        import jax, jax.numpy as jnp
        import numpy as np
        ALPHA = 0.2
        NEG_INF = -9000000000000000.0
        key = jax.random.key(seed)
        k1, k2, k3, k4 = jax.random.split(key, 4)
        N, F_in, F_out = (4096, 128, 128)
        x = jax.random.normal(k1, (N, F_in), dtype=jnp.float32)
        adj = jax.random.randint(k2, (N, N), 0, 2, dtype=jnp.int32)
        W = jax.random.normal(k3, (F_in, F_out), dtype=jnp.float32) * (1.0 / np.sqrt(F_in))
        a = jax.random.normal(k4, (2 * F_out, 1), dtype=jnp.float32) * 0.05
        return {'x': x, 'adj': adj, 'W': W, 'a': a}
    _L0_gnn_all = _L0_gnn_setup()
    _L0_gnn_in = {k: v for k, v in _L0_gnn_all.items() if k in ('W', 'a')}
    del _L0_gnn_all
    return {'x': x, 'adj': adj, 'L0_gnn_W': _L0_gnn_in['W'], 'L0_gnn_a': _L0_gnn_in['a']}

def reference(x, adj, L0_gnn_W, L0_gnn_a):
    import jax
    import jax.numpy as jnp

    def _L0_gnn_ref(x, adj, W, a):
        import jax, jax.numpy as jnp
        import numpy as np
        ALPHA = 0.2
        NEG_INF = -9000000000000000.0
        h = x @ W
        F_out = h.shape[1]
        a1 = a[:F_out, 0]
        a2 = a[F_out:, 0]
        s1 = h @ a1
        s2 = h @ a2
        e = jax.nn.leaky_relu(s1[:, None] + s2[None, :], negative_slope=ALPHA)
        scores = jnp.where(adj > 0, e, NEG_INF)
        attention = jax.nn.softmax(scores, axis=1)
        h_prime = attention @ h
        return jax.nn.elu(h_prime)
    h = jnp.maximum(_layernorm(x, axis=-1), 0.0)
    x = x + _L0_gnn_ref(h, adj, L0_gnn_W, L0_gnn_a)
    return x

_drawn_inputs = setup_inputs


def setup_inputs(seed=0):
    import zlib

    import numpy as np

    out = dict(_drawn_inputs(seed))
    spreads = {}
    factors = {}
    for name, (base, spread) in spreads.items():
        noise = np.random.default_rng([zlib.crc32(name.encode()), seed]).standard_normal(out[name].shape)
        drawn = base * np.exp(spread * noise) if base else spread * noise
        out[name] = jnp.asarray(drawn.astype(out[name].dtype))
    for name, factor in factors.items():
        out[name] = (out[name] * factor).astype(out[name].dtype)
    return out
```

```python
import concourse.bass as bass
from concourse import mybir
from contextlib import ExitStack


def gat_kernel(nc: bass.Bass, x: bass.AP, adj: bass.AP, adjT: bass.AP, W: bass.AP, wT: bass.AP, a: bass.AP,
               out: bass.AP):
    import math

    fp32 = mybir.dt.float32
    fp16 = mybir.dt.float16
    bf16 = mybir.dt.bfloat16
    i32 = mybir.dt.int32
    ALU = mybir.AluOpType
    ACT = mybir.ActivationFunctionType
    AX = mybir.AxisListType

    P = 128
    N, F = x.shape
    T = N // P
    GT = 4
    G = T // GT
    GC = GT * P
    ST = 8
    S = T // ST
    SC = ST * P
    U = T // GT
    UC = GT * SC
    R = 4
    D = F + 1
    EPS = 1e-5
    SLOPE = 0.2
    NEG = -9000000000000000.0
    LIFT = 2.0 ** 96
    LOGTOP = 12 * math.log(2.0)
    GSCALE = 1024.0
    WINDOW = 6.0
    NORM2_MAX, NORM2_MIN = 30.0, 2.0 ** -8
    TRUNC = 1.0 - 2.0 ** -11

    x_v = x.rearrange("(p t) f -> p t f", p=P)
    out_v = out.rearrange("(p t) f -> p t f", p=P)
    adj_v = adj.rearrange("(p t) n -> t p n", p=P)

    ctx = ExitStack()
    with ctx:
        def sb(name, shape, dt=fp32):
            return ctx.enter_context(nc.sbuf_tensor(name, shape, dt))

        def sem(name):
            return ctx.enter_context(nc.semaphore(name))

        xs = sb("xs", [P, T, F])
        ww = sb("ww", [P, F + 2])
        wT_sb = sb("wT_sb", [P, F])
        a_sb = sb("a_sb", [P, 2])
        wa_bc = sb("wa_bc", [P, P])
        ident = sb("ident", [P, P])
        ones = sb("ones", [P, P])
        bst = sb("bst", [P, T, 6])
        mv = sb("mv", [P, T, 2])
        std = sb("std", [P, T])
        rstd = sb("rstd", [P, T])
        ysum = sb("ysum", [P, G + 1])
        ysum_bc = sb("ysum_bc", [P, P])
        hsum = sb("hsum", [P, F])
        hs = sb("hs", [P, T, D])
        sc = sb("sc", [P, T, 2])
        st = sb("st", [P, 4])
        m5 = sb("m5", [P, 1])
        diag = sb("diag", [4, 4])
        mx = sb("mx", [P, 4])
        bias_cq = sb("bias_cq", [P, 1])
        neg_m2 = sb("neg_m2", [P, 1])
        viol = sb("viol", [P, 4])
        flag = sb("flag", [P, 1], i32)
        sq = sb("sq", [P, F])
        cp = sb("cp", [P, N])
        qf = sb("qf", [P, T])
        qp = sb("qp", [P, T])
        vf = sb("vf", [P, T])
        gf = sb("gf", [P, 2, GT, D])
        gs = sb("gs", [P, T, 2 * D], fp16)
        ring = sb("ring", [P, R, UC], i32)
        mask = sb("mask", [P, 2, UC], bf16)
        w = sb("w", [P, 2, GT, SC])
        xn = w[:, 0, 0, :].rearrange("p (g k f) -> p g k f", g=2, k=GT)
        yT = w[:, 0, 1, :].rearrange("p (g n) -> p g n", g=2)
        zt = sb("zt", [P, ST])
        rt = sb("rt", [P, ST])
        late = sb("late", [P, ST * (2 * D + 2 * F)])
        s1_bc = late[:, 0:N]
        acc = late[:, 0:ST * 2 * D].rearrange("p (k c) -> p k c", k=ST)
        res = late[:, ST * 2 * D:ST * (2 * D + F)].rearrange("p (k c) -> p k c", k=ST)
        en = late[:, ST * (2 * D + F):ST * (2 * D + 2 * F)].rearrange("p (k c) -> p k c", k=ST)

        row_adj = ring[:, 0, :]
        scores = w[:, 0, :, :].rearrange("p b n -> p (b n)")
        penalty = w[:, 1, :, :].rearrange("p b n -> p (b n)")
        scores_t = scores.rearrange("p (q t) -> p t q", t=T)
        s2_bc = cp[:, :]
        s2_bc_t = cp[:, :].rearrange("p (q t) -> p t q", t=T)
        probs_T = late[:, 0:GC]
        g_hp = late[:, GC:GC + F]
        g_en = late[:, GC + F:GC + 2 * F]
        g_res = late[:, GC + 2 * F:GC + 3 * F]
        g_cols = late[:, GC + 3 * F:GC + 3 * F + 4]
        neg_max, den = g_cols[:, 0:1], g_cols[:, 1:2]

        ps = ctx.enter_context(nc.psum_tensor("ps", [P, 8, 512], fp32))

        cp16 = cp[:, :].bitcast(fp16).rearrange("p (n h) -> p n h", h=2)
        qp16 = qp[:, :].bitcast(fp16).rearrange("p (n h) -> p n h", h=2)
        w16 = [[w[:, k, b, :].bitcast(fp16).rearrange("p (n h) -> p n h", h=2) for b in range(GT)] for k in range(2)]

        x_in = [sem(f"x_in{c}") for c in range(4)]
        w_in = sem("w_in")
        adj_in = [sem(f"adj_in{k}") for k in range(R)]
        out_done = sem("out_done")
        ident_zero = sem("ident_zero")
        ident_ready = sem("ident_ready")
        wa_mm = sem("wa_mm")
        ww_ready = sem("ww_ready")
        norm_ready = sem("norm_ready")
        dve_step = sem("dve_step")
        act_step = sem("act_step")
        pool_step = sem("pool_step")
        var_ready = sem("var_ready")
        std_ready = sem("std_ready")
        xn_ready = sem("xn_ready")
        xT_ready = sem("xT_ready")
        yT_ready = sem("yT_ready")
        h_mm = sem("h_mm")
        s1_mm = sem("s1_mm")
        h_ready = sem("h_ready")
        s1_ready = sem("s1_ready")
        ysum_ready = sem("ysum_ready")
        hsum_mm = sem("hsum_mm")
        hsum_ready = sem("hsum_ready")
        st_ready = sem("st_ready")
        st_t = sem("st_t")
        diag_ready = sem("diag_ready")
        mx_mm = sem("mx_mm")
        bias_ready = sem("bias_ready")
        flag_ready = sem("flag_ready")
        v_ready = sem("v_ready")
        qc_hi = sem("qc_hi")
        qc_ready = sem("qc_ready")
        gf_ready = sem("gf_ready")
        g_hi = sem("g_hi")
        g_ready = sem("g_ready")
        mask_ready = sem("mask_ready")
        w_ready = sem("w_ready")
        w_used = sem("w_used")
        acc_done = sem("acc_done")
        evac_a = sem("evac_a")
        evac_d = sem("evac_d")
        t_ready = sem("t_ready")
        r_ready = sem("r_ready")
        hp_ready = sem("hp_ready")
        hz_ready = sem("hz_ready")
        en_ready = sem("en_ready")
        res_ready = sem("res_ready")
        gen_col = sem("gen_col")
        gen_row = sem("gen_row")
        gen_s2 = sem("gen_s2")
        gen_adj = sem("gen_adj")
        gen_step = sem("gen_step")
        gen_scores = sem("gen_scores")
        gen_probs = sem("gen_probs")
        gen_turned = sem("gen_turned")
        gen_copied = sem("gen_copied")
        gen_num = sem("gen_num")
        gen_min = sem("gen_min")
        gen_exp = sem("gen_exp")
        gen_res = sem("gen_res")
        gen_out = sem("gen_out")

        block = ctx.enter_context(nc.Block())

        def chosen(eng):
            eng.wait_ge(flag_ready, 1)
            return eng.value_load(flag[0:1, 0:1], min_val=0, max_val=1)

        @block.sync
        def _(sp):
            for c in range(4):
                sp.dma_start(xs[:, c * 8:(c + 1) * 8, :], x_v[:, c * 8:(c + 1) * 8, :]).then_inc(x_in[c], 16)
            for k in range(R):
                sp.dma_start(ring[:, k, :], adjT[k // U, k % U]).then_inc(adj_in[k], 16)
            adj_units = adjT.rearrange("s u p n -> (s u) p n")
            general = chosen(sp)
            with sp.If(general == 0):
                with sp.Fori(1, S * U // R) as r:
                    for k in range(R):
                        sp.wait_ge(mask_ready, r * R + (k - R + 1))
                        sp.dma_start(ring[:, k, :], adj_units[r * R + k]).then_inc(adj_in[k], 16)
            with sp.If(general == 1):
                for k in range(R):
                    sp.wait_ge(adj_in[k], 16)
                sp.dma_start(row_adj, adj_v[0]).then_inc(gen_adj, 16)
                with sp.Fori(1, T) as t:
                    sp.wait_ge(gen_scores, t)
                    sp.dma_start(row_adj, adj_v[t]).then_inc(gen_adj, 16)

        @block.gpsimd
        def _(pool):
            nc.gpsimd.memset(ones[:, :], 1.0)
            nc.gpsimd.memset(hs[:, :, F:D], 1.0)
            nc.gpsimd.memset(ident[:, :], 0.0).then_inc(ident_zero, 1)
            pool.wait_ge(ident_zero, 1)
            nc.gpsimd.affine_select(out=ident[:, :], in_=ident[:, :], compare_op=ALU.not_equal, fill=1.0,
                                    base=0, pattern=[[-1, P]], channel_multiplier=1).then_inc(ident_ready, 1)
            general = chosen(pool)
            with pool.If(general == 0):
                pool.wait_ge(v_ready, 1)
                for u in range(U):
                    if u >= 2:
                        pool.wait_ge(g_ready, u - 1)
                    for k in range(GT):
                        t = u * GT + k
                        last = nc.gpsimd.tensor_scalar(gf[:, u % 2, k, :], hs[:, t, :], vf[:, t:t + 1], GSCALE,
                                                       ALU.mult, ALU.mult)
                    last.then_inc(gf_ready, 1)
                    pool.wait_ge(g_hi, u + 1)
                    nc.gpsimd.tensor_tensor(gs[:, u * GT:(u + 1) * GT, D:2 * D], gf[:, u % 2, :, :],
                                            gs[:, u * GT:(u + 1) * GT, 0:D], ALU.subtract).then_inc(g_ready, 1)
                with pool.Fori(0, S) as s:
                    pool.wait_ge(res_ready, s + 1)
                    pool.dma_start(out_v[:, bass.ds(s * ST, ST), :], res[:, :, :]).then_inc(out_done, 16)
                pool.wait_ge(out_done, 16 * S)
            with pool.If(general == 1):
                with pool.Fori(0, T) as t:
                    pool.wait_ge(gen_res, t + 1)
                    pool.dma_start(out_v[:, bass.ds(t, 1), :], g_res.unsqueeze(1)).then_inc(gen_out, 16)
                pool.wait_ge(gen_out, 16 * T)

        @block.tensor
        def _(pe):
            pe.wait_ge(w_in, 48)
            nc.tensor.matmul(ps[:, 7, 0:2], wT_sb[:, :], a_sb[:, :], start=True, stop=True).then_inc(wa_mm, 1)
            pe.wait_ge(ident_ready, 1)

            def transposes(g):
                pe.wait_ge(xn_ready, g + 1)
                if g >= 2:
                    pe.wait_ge(yT_ready, g - 1)
                for k in range(GT):
                    last = nc.tensor.transpose(ps[:, g % 2, k * P:(k + 1) * P], xn[:, g % 2, k, :], ident[:, :])
                last.then_inc(xT_ready, 1)

            transposes(0)
            pe.wait_ge(ww_ready, 1)
            for g in range(G):
                if g + 1 < G:
                    transposes(g + 1)
                pe.wait_ge(yT_ready, g + 1)
                if g >= 2:
                    pe.wait_ge(s1_ready, g - 1)
                nc.tensor.matmul(ps[:, 6 + g % 2, :], wa_bc[:, :], yT[:, g % 2, :], start=True,
                                 stop=True).then_inc(s1_mm, 1)
                if g >= 2:
                    pe.wait_ge(h_ready, g - 1)
                for k in range(GT):
                    last = nc.tensor.matmul(ps[:, 2 + 2 * (g % 2) + k // 2, (k % 2) * 256:(k % 2) * 256 + F + 2],
                                            yT[:, g % 2, k * P:(k + 1) * P], ww[:, :], start=True, stop=True)
                last.then_inc(h_mm, 1)
            pe.wait_ge(st_ready, 1)
            pe.wait_ge(norm_ready, 1)
            nc.tensor.transpose(ps[0:4, 0, 0:P], st[:, :], ident[:, :]).then_inc(st_t, 1)
            pe.wait_ge(diag_ready, 1)
            nc.tensor.matmul(ps[:, 1, 0:4], ones[0:4, :], diag[:, :], start=True, stop=True).then_inc(mx_mm, 1)
            pe.wait_ge(ysum_ready, 1)
            pe.wait_ge(s1_ready, G)
            nc.tensor.matmul(ps[:, 7, 0:F], ysum_bc[:, :], ww[:, 0:F], start=True, stop=True).then_inc(hsum_mm, 1)
            pe.wait_ge(hsum_ready, 1)
            pe.wait_ge(h_ready, G)
            pe.wait_ge(bias_ready, 1)

            def super_tile(s, first):
                for u in range(U):
                    if first:
                        pe.wait_ge(g_ready, u + 1)
                    for b in range(GT):
                        pe.wait_ge(w_ready, (s * U + u) * GT + b + 1)
                        jb = u * GT + b
                        for i in range(ST):
                            if jb == 0 and not first:
                                if i % 2 == 0:
                                    pe.wait_ge(evac_a, (s - 1) * 4 + i // 2 + 1)
                                else:
                                    pe.wait_ge(evac_d, (s - 1) * 4 + i // 2 + 1)
                            hi = w16[u % 2][b][:, i * P:(i + 1) * P, 1]
                            lo = w16[u % 2][b][:, i * P:(i + 1) * P, 0]
                            nc.tensor.matmul(ps[:, i, 0:2 * D], hi, gs[:, jb, :], start=(jb == 0), stop=False)
                            last = nc.tensor.matmul(ps[:, i, 0:D], lo, gs[:, jb, 0:D], start=False,
                                                    stop=(jb == T - 1))
                            if jb == T - 1:
                                last.then_inc(acc_done, 1)
                    if u < U - 1:
                        last.then_inc(w_used, 1)

            general = chosen(pe)
            with pe.If(general == 0):
                super_tile(0, True)
                with pe.Fori(1, S) as s:
                    super_tile(s, False)
            with pe.If(general == 1):
                with pe.Fori(0, T) as t:
                    pe.wait_ge(gen_col, t + 1)
                    nc.tensor.matmul(ps[:, 0, 0:P], sq[:, :], ident[:, :], start=True, stop=True).then_inc(gen_row, 1)
                with pe.Fori(0, T) as t:
                    pe.wait_ge(gen_probs, t + 1)
                    for g in range(G):
                        for k in range(GT):
                            last = nc.tensor.transpose(ps[:, 0, k * P:(k + 1) * P], scores_t[:, g * GT + k, :],
                                                       ident[:, :])
                        last.then_inc(gen_turned, 1)
                        pe.wait_ge(gen_copied, t * G + (g + 1))
                        for k in range(GT):
                            j = g * GT + k
                            last = nc.tensor.matmul(ps[:, 1, 0:F], probs_T[:, k * P:(k + 1) * P], hs[:, j, 0:F],
                                                    start=(j == 0), stop=(j == T - 1))
                    last.then_inc(gen_num, 1)

        @block.scalar
        def _(act):
            act.dma_start(wT_sb[:, :], wT).then_inc(w_in, 16)
            act.dma_start(ww[:, 0:F], W).then_inc(w_in, 16)
            act.dma_start(a_sb[:, :], a).then_inc(w_in, 16)
            act.wait_ge(w_in, 48)
            nc.scalar.activation(sq[:, :], wT_sb[:, :], ACT.Square, accum_out=st[:, 3:4]).then_inc(norm_ready, 1)

            def deviations(c):
                act.wait_ge(var_ready, c + 1)
                nc.scalar.activation(std[:, c * 8:(c + 1) * 8], mv[:, c * 8:(c + 1) * 8, 1], ACT.Sqrt,
                                     bias=EPS).then_inc(std_ready, 1)

            deviations(0)
            for c in range(4):
                if c < 3:
                    deviations(c + 1)
                for g in (2 * c, 2 * c + 1):
                    act.wait_ge(xT_ready, g + 1)
                    if g >= 2:
                        act.wait_ge(h_mm, g - 1)
                    nc.scalar.activation(yT[:, g % 2, :], ps[:, g % 2, :], ACT.Relu,
                                         accum_out=ysum[:, g:g + 1]).then_inc(yT_ready, 1)
                    act.wait_ge(s1_mm, g + 1)
                    nc.scalar.copy(s1_bc[:, g * GC:(g + 1) * GC], ps[:, 6 + g % 2, :]).then_inc(s1_ready, 1)
            act.wait_ge(bias_ready, 1)
            act.wait_ge(s1_ready, G)
            nc.scalar.activation(vf[:, :], sc[:, :, 1], ACT.Exp, bias=neg_m2[:, :]).then_inc(v_ready, 1)
            nc.scalar.activation(qf[:, :], sc[:, :, 1], ACT.Exp, bias=bias_cq[:, :],
                                 scale=SLOPE - 1.0).then_inc(act_step, 1)
            act.wait_ge(act_step, 1)
            nc.scalar.mul(qp16[:, :, 1], qf[:, :], TRUNC).then_inc(qc_hi, 1)
            for s in range(S):
                nc.scalar.activation(s1_bc[:, s * SC:(s + 1) * SC], s1_bc[:, s * SC:(s + 1) * SC], ACT.Exp,
                                     bias=bias_cq[:, :], scale=1.0 - SLOPE).then_inc(act_step, 1)
                act.wait_ge(act_step, s + 2)
                nc.scalar.mul(cp16[:, s * SC:(s + 1) * SC, 1], s1_bc[:, s * SC:(s + 1) * SC],
                              TRUNC).then_inc(qc_hi, 1)

            def g_high(u):
                act.wait_ge(gf_ready, u + 1)
                nc.scalar.copy(gs[:, u * GT:(u + 1) * GT, 0:D], gf[:, u % 2, :, :]).then_inc(g_hi, 1)

            def finish(s):
                for i in range(0, ST, 2):
                    act.wait_ge(acc_done, s * ST + i + 1)
                    nc.scalar.copy(acc[:, i, :], ps[:, i, 0:2 * D]).then_inc(evac_a, 1)
                act.wait_ge(r_ready, s + 1)
                for i in range(ST):
                    last = nc.scalar.mul(en[:, i, :], acc[:, i, 0:F], rt[:, i:i + 1])
                last.then_inc(hp_ready, 1)
                act.wait_ge(hz_ready, s + 1)
                nc.scalar.activation(en[:, :, :], en[:, :, :], ACT.Exp).then_inc(en_ready, 1)

            def units(s, first):
                for u in range(U):
                    if first:
                        g_high(u)
                    act.wait_ge(adj_in[u % R], 16 * (s * (U // R) + u // R + 1))
                    if not (first and u < 2):
                        act.wait_ge(w_ready, (s * U + u - 1) * GT)
                    nc.scalar.activation(mask[:, u % 2, :], ring[:, u % R, :], ACT.Relu,
                                         scale=LIFT).then_inc(mask_ready, 1)
                    if u == 1 and not first:
                        finish(s - 1)

            general = chosen(act)
            with act.If(general == 0):
                units(0, True)
                with act.Fori(1, S) as s:
                    units(s, False)
                finish(S - 1)
            with act.If(general == 1):
                with act.Fori(0, T) as t:
                    act.wait_ge(gen_scores, t + 1)
                    nc.scalar.activation(scores, scores, ACT.Exp, bias=neg_max, accum_out=den).then_inc(gen_probs, 1)
                    for g in range(G):
                        act.wait_ge(gen_turned, t * G + (g + 1))
                        nc.scalar.copy(probs_T, ps[:, 0, :]).then_inc(gen_copied, 1)
                    act.wait_ge(gen_min, t + 1)
                    nc.scalar.activation(g_en, g_en, ACT.Exp).then_inc(gen_exp, 1)

        @block.vector
        def _(dve):
            steps = [0]

            def step(ins):
                steps[0] += 1
                ins.then_inc(dve_step, 1)
                dve.wait_ge(dve_step, steps[0])

            dve.wait_ge(wa_mm, 1)
            step(nc.vector.tensor_copy(ww[:, F:F + 2], ps[:, 7, 0:2]))
            nc.vector.tensor_copy(wa_bc[:, :], ww[:, F:F + 1].to_broadcast([P, P])).then_inc(ww_ready, 1)

            def stats(c):
                dve.wait_ge(x_in[c], 16)
                for t in range(c * 8, c * 8 + 8):
                    last = nc.vector.bn_stats(bst[:, t, :], xs[:, t, :])
                step(last)
                for t in range(c * 8, c * 8 + 8):
                    last = nc.vector.bn_aggr(mv[:, t, :], bst[:, t, :])
                last.then_inc(var_ready, 1)

            def evac_h(g):
                dve.wait_ge(h_mm, g + 1)
                v = ps[:, 2 + 2 * (g % 2):4 + 2 * (g % 2), :].rearrange("p b (k c) -> p (b k) c", k=2)
                nc.vector.tensor_copy(hs[:, g * GT:(g + 1) * GT, 0:F], v[:, :, 0:F])
                nc.vector.tensor_copy(sc[:, g * GT:(g + 1) * GT, :], v[:, :, F:F + 2]).then_inc(h_ready, 1)

            stats(0)
            for c in range(4):
                if c < 3:
                    stats(c + 1)
                dve.wait_ge(std_ready, c + 1)
                step(nc.vector.reciprocal(rstd[:, c * 8:(c + 1) * 8], std[:, c * 8:(c + 1) * 8]))
                for g in (2 * c, 2 * c + 1):
                    if g >= 2:
                        dve.wait_ge(xT_ready, g - 1)
                    for k in range(GT):
                        t = g * GT + k
                        last = nc.vector.tensor_scalar(xn[:, g % 2, k, :], xs[:, t, :], mv[:, t, 0:1],
                                                       rstd[:, t:t + 1], ALU.subtract, ALU.mult)
                    last.then_inc(xn_ready, 1)
                    if g >= 1:
                        evac_h(g - 1)
            evac_h(G - 1)
            dve.wait_ge(h_ready, G)
            nc.vector.reduce_max(st[:, 0:2], sc[:, :, :].rearrange("p t c -> p c t"), AX.X)
            step(nc.vector.tensor_reduce(m5[:, :], sc[:, :, 1], AX.X, ALU.min))
            nc.vector.tensor_scalar(st[:, 2:3], m5[:, :], -1.0, None, ALU.mult).then_inc(st_ready, 1)
            dve.wait_ge(st_t, 1)
            step(nc.vector.reduce_max(m5[0:4, :], ps[0:4, 0, 0:P], AX.X))
            nc.vector.tensor_scalar(diag[:, :], ident[0:4, 0:4], m5[0:4, :], None, ALU.mult).then_inc(diag_ready, 1)
            dve.wait_ge(mx_mm, 1)
            step(nc.vector.tensor_copy(mx[:, :], ps[:, 1, 0:4]))
            step(nc.vector.tensor_tensor(viol[:, 0:1], mx[:, 0:1], mx[:, 2:3], ALU.max))
            nc.vector.tensor_scalar(bias_cq[:, :], viol[:, 0:1], SLOPE - 1.0, LOGTOP, ALU.mult, ALU.add)
            nc.vector.tensor_scalar(neg_m2[:, :], mx[:, 1:2], -1.0, None, ALU.mult).then_inc(bias_ready, 1)
            step(nc.vector.tensor_tensor(viol[:, 1:2], viol[:, 0:1], mx[:, 1:2], ALU.add))
            nc.vector.tensor_scalar(viol[:, 1:2], viol[:, 1:2], 1.0 - SLOPE, -WINDOW, ALU.mult, ALU.add)
            nc.vector.tensor_scalar(viol[:, 2:3], mx[:, 3:4], -NORM2_MAX, None, ALU.add)
            step(nc.vector.tensor_scalar(viol[:, 3:4], mx[:, 3:4], -1.0, NORM2_MIN, ALU.mult, ALU.add))
            step(nc.vector.reduce_max(m5[:, :], viol[:, 1:4], AX.X))
            nc.vector.tensor_scalar(flag[:, :], m5[:, :], 0.0, None, ALU.is_gt).then_inc(flag_ready, 1)
            dve.wait_ge(yT_ready, G)
            step(nc.vector.reduce_sum(ysum[:, G:G + 1], ysum[:, 0:G], AX.X))
            nc.vector.tensor_copy(ysum_bc[:, :], ysum[:, G:G + 1].to_broadcast([P, P])).then_inc(ysum_ready, 1)
            dve.wait_ge(qc_hi, 1)
            nc.vector.tensor_tensor(qp16[:, :, 0], qf[:, :], qp16[:, :, 1], ALU.subtract)
            dve.wait_ge(hsum_mm, 1)
            nc.vector.tensor_scalar(hsum[:, :], ps[:, 7, 0:F], 1.0 / N, None, ALU.mult).then_inc(hsum_ready, 1)
            for s in range(S):
                dve.wait_ge(qc_hi, s + 2)
                nc.vector.tensor_tensor(cp16[:, s * SC:(s + 1) * SC, 0], s1_bc[:, s * SC:(s + 1) * SC],
                                        cp16[:, s * SC:(s + 1) * SC, 1], ALU.subtract).then_inc(qc_ready, 1)
            dve.wait_ge(qc_ready, S)

            def evacuate(s):
                for i in range(1, ST, 2):
                    dve.wait_ge(acc_done, s * ST + i + 1)
                    nc.vector.tensor_copy(acc[:, i, :], ps[:, i, 0:2 * D]).then_inc(evac_d, 1)

            def finish(s):
                dve.wait_ge(evac_a, (s + 1) * 4)
                dve.wait_ge(evac_d, (s + 1) * 4)
                nc.vector.tensor_tensor(acc[:, :, 0:D], acc[:, :, 0:D], acc[:, :, D:2 * D],
                                        ALU.add).then_inc(t_ready, 1)
                dve.wait_ge(t_ready, 5 * s + 1)
                nc.vector.tensor_scalar(zt[:, :], acc[:, :, F], 0.0, None, ALU.is_equal).then_inc(t_ready, 1)
                dve.wait_ge(t_ready, 5 * s + 2)
                nc.vector.tensor_tensor(rt[:, :], acc[:, :, F], zt[:, :], ALU.add).then_inc(t_ready, 1)
                dve.wait_ge(t_ready, 5 * s + 3)
                nc.vector.reciprocal(rt[:, :], rt[:, :]).then_inc(r_ready, 1)
                dve.wait_ge(hp_ready, s + 1)
                for i in range(ST):
                    last = nc.vector.scalar_tensor_tensor(acc[:, i, 0:F], hsum[:, :], zt[:, i:i + 1], en[:, i, :],
                                                          ALU.mult, ALU.add)
                last.then_inc(t_ready, 1)
                dve.wait_ge(t_ready, 5 * s + 4)
                nc.vector.tensor_scalar(en[:, :, :], acc[:, :, 0:F], 0.0, None, ALU.min).then_inc(hz_ready, 1)
                dve.wait_ge(en_ready, s + 1)
                nc.vector.scalar_tensor_tensor(acc[:, :, 0:F], acc[:, :, 0:F], 0.0, en[:, :, :], ALU.max,
                                               ALU.add).then_inc(t_ready, 1)
                dve.wait_ge(t_ready, 5 * s + 5)
                nc.vector.scalar_tensor_tensor(res[:, :, :], acc[:, :, 0:F], -1.0, xs[:, bass.ds(s * ST, ST), :],
                                               ALU.add, ALU.add).then_inc(res_ready, 1)

            def units(s, first):
                for u in range(U):
                    dve.wait_ge(mask_ready, s * U + u + 1)
                    if u >= 2:
                        dve.wait_ge(w_used, s * (U - 1) + (u - 1))
                    elif not first and u == 0:
                        dve.wait_ge(w_used, s * (U - 1))
                    elif not first:
                        dve.wait_ge(acc_done, s * ST)
                    for b in range(GT):
                        t = u * GT + b
                        nc.vector.scalar_tensor_tensor(
                            w[:, u % 2, b, :], cp[:, bass.ds(s * SC, SC)], qp[:, t:t + 1],
                            mask[:, u % 2, b * SC:(b + 1) * SC], ALU.max, ALU.min).then_inc(w_ready, 1)
                    if not first and u == 0:
                        evacuate(s - 1)
                    if not first and u == 1:
                        finish(s - 1)
                    if not first and u == U - 1:
                        dve.wait_ge(out_done, 16 * s)
            general = chosen(dve)
            with dve.If(general == 0):
                units(0, True)
                with dve.Fori(1, S) as s:
                    units(s, False)
                evacuate(S - 1)
                finish(S - 1)
            with dve.If(general == 1):
                with dve.Fori(0, T) as t:
                    nc.vector.tensor_copy(sq[:, :], sc[:, bass.ds(t, 1), 1].to_broadcast([P, P])).then_inc(gen_col, 1)
                    dve.wait_ge(gen_row, t + 1)
                    nc.vector.tensor_copy(s2_bc_t[:, bass.ds(t, 1), :],
                                          ps[:, 0, 0:P].unsqueeze(1)).then_inc(gen_s2, 1)
                    dve.wait_ge(gen_s2, t + 1)
                STEPS = 7

                def row_tile(t, first):
                    done = [0]

                    def gstep(ins):
                        done[0] += 1
                        ins.then_inc(gen_step, 1)
                        dve.wait_ge(gen_step, t * STEPS + done[0])

                    dve.wait_ge(gen_adj, 16 * (t + 1))
                    nc.vector.tensor_scalar(penalty, row_adj, 0.0, NEG, ALU.is_le, ALU.mult)
                    gstep(nc.vector.tensor_scalar(scores, s2_bc, sc[:, bass.ds(t, 1), 0], None, ALU.add))
                    gstep(nc.vector.scalar_tensor_tensor(scores, scores, SLOPE, scores, ALU.mult, ALU.max))
                    gstep(nc.vector.tensor_tensor(scores, scores, penalty, ALU.add))
                    gstep(nc.vector.reduce_max(g_cols[:, 2:3], scores, AX.X))
                    nc.vector.tensor_scalar(neg_max, g_cols[:, 2:3], -1.0, None, ALU.mult).then_inc(gen_scores, 1)
                    dve.wait_ge(gen_probs, t + 1)
                    gstep(nc.vector.reciprocal(g_cols[:, 3:4], den))
                    dve.wait_ge(gen_num, t + 1)
                    if not first:
                        dve.wait_ge(gen_out, 16 * t)
                    gstep(nc.vector.tensor_scalar(g_hp, ps[:, 1, 0:F], g_cols[:, 3:4], None, ALU.mult))
                    nc.vector.tensor_scalar(g_en, g_hp, 0.0, None, ALU.min).then_inc(gen_min, 1)
                    dve.wait_ge(gen_exp, t + 1)
                    gstep(nc.vector.scalar_tensor_tensor(g_hp, g_hp, 0.0, g_en, ALU.max, ALU.add))
                    nc.vector.scalar_tensor_tensor(g_res.unsqueeze(1), g_hp.unsqueeze(1), -1.0,
                                                   xs[:, bass.ds(t, 1), :], ALU.add, ALU.add).then_inc(gen_res, 1)

                row_tile(0, True)
                with dve.Fori(1, T) as t:
                    row_tile(t, False)

    return nc


def kernel(x, adj, L0_gnn_W, L0_gnn_a):
    import numpy as _np
    import concourse.bacc as _bacc
    from concourse import mybir as _mybir
    from concourse.bass_utils import run_bass_kernel_spmd as _run

    nc = _bacc.Bacc("TRN2", target_bir_lowering=False, num_devices=1)
    x, adj, W, a = (_np.asarray(v) for v in (x, adj, L0_gnn_W, L0_gnn_a))
    blocks = adj.reshape(128, 4, 8, 128, 8, 4).transpose(1, 4, 3, 5, 2, 0).reshape(4, 8, 128, 4096)
    arrays = {
        "x": _np.ascontiguousarray(x),
        "adj": _np.ascontiguousarray(adj),
        "adjT": _np.ascontiguousarray(blocks),
        "W": _np.ascontiguousarray(W),
        "wT": _np.ascontiguousarray(W.T),
        "a": _np.ascontiguousarray(a.reshape(2, 128).T),
    }
    args = [nc.dram_tensor(f"in_{n}", v.shape, _mybir.dt.from_np(v.dtype), kind="ExternalInput").ap()
            for n, v in arrays.items()]
    args.append(nc.dram_tensor("out", x.shape, _mybir.dt.float32, kind="ExternalOutput").ap())
    gat_kernel(nc, *args)
    r = _run(nc, [{f"in_{n}": v for n, v in arrays.items()}], core_ids=[0])
    return r.results[0]["out"]
```

```python
import concourse.bass as bass
from concourse import mybir
from contextlib import ExitStack


def gat_kernel(nc: bass.Bass, x: bass.AP, adj: bass.AP, adjT: bass.AP, W: bass.AP, wT: bass.AP, a: bass.AP,
               out: bass.AP):
    import math

    fp32 = mybir.dt.float32
    fp16 = mybir.dt.float16
    bf16 = mybir.dt.bfloat16
    i32 = mybir.dt.int32
    ALU = mybir.AluOpType
    ACT = mybir.ActivationFunctionType
    AX = mybir.AxisListType

    P = 128
    N, F = x.shape
    T = N // P
    GT = 4
    G = T // GT
    GC = GT * P
    CT = 8
    C = T // CT
    ST = 8
    S = T // ST
    SC = ST * P
    HB = ST // 2
    PB = 2
    Q = T // PB
    PC = PB * SC
    R = 8
    MR = 4
    WR = 8
    D = F + 1
    EPS = 1e-5
    SLOPE = 0.2
    NEG = -9000000000000000.0
    LIFT = 2.0 ** 96
    LOGTOP = 12 * math.log(2.0)
    GSCALE = 1024.0
    TRUNC = 1.0 - 2.0 ** -11
    TINY = 2.0 ** -80
    WINDOW = 6.0
    NORM2_MAX, NORM2_MIN = 30.0, 2.0 ** -8

    x_v = x.rearrange("(p t) f -> p t f", p=P)
    out_v = out.rearrange("(p t) f -> p t f", p=P)
    adj_v = adj.rearrange("(p t) n -> t p n", p=P)

    ctx = ExitStack()
    with ctx:
        def sb(name, shape, dt=fp32):
            return ctx.enter_context(nc.sbuf_tensor(name, shape, dt))

        def sem(name):
            return ctx.enter_context(nc.semaphore(name))

        xs = sb("xs", [P, T, F])
        ww = sb("ww", [P, F + 2])
        wT_sb = sb("wT_sb", [P, F])
        a_sb = sb("a_sb", [P, 2])
        ident = sb("ident", [P, P])
        ones = sb("ones", [P, P])
        bst = sb("bst", [P, T, 6])
        mv = sb("mv", [P, T, 2])
        std = sb("std", [P, T])
        rstd = sb("rstd", [P, T])
        ysum = sb("ysum", [P, G + 1])
        square = sb("square", [P, P])
        hsum = sb("hsum", [P, D])
        rest = sb("rest", [P, D])
        hsum_part = sb("hsum_part", [P, 3, D], bf16)
        hsum_rows = sb("hsum_rows", [96, D], bf16)
        tiny = sb("tiny", [96, P], bf16)
        hs = sb("hs", [P, T, F + 2])
        sc = sb("sc", [P, T, 2])
        st = sb("st", [P, 4])
        m5 = sb("m5", [P, 1])
        diag = sb("diag", [4, 4])
        mx = sb("mx", [P, 4])
        bias_cq = sb("bias_cq", [P, 1])
        neg_m2 = sb("neg_m2", [P, 1])
        viol = sb("viol", [P, 4])
        flag = sb("flag", [P, 1], i32)
        cqf = sb("cqf", [P, 2, T])
        cqp = sb("cqp", [P, 2, T])
        vf = sb("vf", [P, T])
        cp = sb("cp", [P, N])
        gf = sb("gf", [P, 2, GT, D])
        gs = sb("gs", [P, T, 2 * D], fp16)
        ring = sb("ring", [P, R, PC], i32)
        mask = sb("mask", [P, MR, PC], bf16)
        w = sb("w", [P, WR, SC])
        XN = 4
        xn = w[:, 0:2, :].rearrange("p b (g k f) -> p (b g) k f", g=2, k=GT)
        yT = w[:, 2, :].rearrange("p (g n) -> p g n", g=2)
        acc = sb("acc", [P, ST, D])
        rt = sb("rt", [P, ST])
        res = sb("res", [P, ST, F])
        en = sb("en", [P, ST, F])
        late = w[:, 7, :]

        row_adj = ring[:, 0:2, :].rearrange("p k n -> p (k n)")
        scores = w[:, 0:4, :].rearrange("p b n -> p (b n)")
        penalty = ring[:, 2:4, :].rearrange("p k n -> p (k n)").bitcast(fp32)
        scores_t = scores.rearrange("p (q t) -> p t q", t=T)
        s2_bc = cp[:, :]
        s2_bc_t = cp[:, :].rearrange("p (q t) -> p t q", t=T)
        probs_T = late[:, 0:GC]
        g_hp = late[:, GC:GC + F]
        g_en = late[:, GC + F:GC + 2 * F]
        g_res = late[:, GC + 2 * F:GC + 3 * F]
        g_cols = late[:, GC + 3 * F:GC + 3 * F + 4]
        neg_max, den = g_cols[:, 0:1], g_cols[:, 1:2]

        ps = ctx.enter_context(nc.psum_tensor("ps", [P, 8, 512], fp32))

        cqp16 = cqp[:, :, :].bitcast(fp16).rearrange("p c (n h) -> p c n h", h=2)
        w16 = [w[:, k, :].bitcast(fp16).rearrange("p (n h) -> p n h", h=2) for k in range(WR)]

        x_in = [sem(f"x_in{c}") for c in range(C)]
        w_in = sem("w_in")
        adj_in = [sem(f"adj_in{k}") for k in range(R)]
        out_done = sem("out_done")
        ident_zero = sem("ident_zero")
        ident_ready = sem("ident_ready")
        wa_mm = sem("wa_mm")
        ww_ready = sem("ww_ready")
        norm_ready = sem("norm_ready")
        dve_step = sem("dve_step")
        act_step = sem("act_step")
        pool_step = sem("pool_step")
        var_ready = sem("var_ready")
        std_ready = sem("std_ready")
        rstd_ready = sem("rstd_ready")
        xn_pool = sem("xn_pool")
        xn_dve = sem("xn_dve")
        xT_ready = sem("xT_ready")
        yT_ready = sem("yT_ready")
        h_mm = sem("h_mm")
        h_ready = sem("h_ready")
        ysum_ready = sem("ysum_ready")
        hsum_mm = sem("hsum_mm")
        hsum_ready = sem("hsum_ready")
        hrows_ready = sem("hrows_ready")
        st_ready = sem("st_ready")
        st_t = sem("st_t")
        diag_ready = sem("diag_ready")
        mx_mm = sem("mx_mm")
        bias_ready = sem("bias_ready")
        flag_ready = sem("flag_ready")
        ones_ready = sem("ones_ready")
        v_ready = sem("v_ready")
        cq_hi = sem("cq_hi")
        cq_ready = sem("cq_ready")
        c_turned = sem("c_turned")
        c_act = sem("c_act")
        c_dve = sem("c_dve")
        gf_ready = sem("gf_ready")
        g_hi = sem("g_hi")
        g_ready = sem("g_ready")
        mask_ready = sem("mask_ready")
        w_ready = sem("w_ready")
        w_used = sem("w_used")
        acc_done = sem("acc_done")
        hi_copied = sem("hi_copied")
        acc_ready = sem("acc_ready")
        fin_step = sem("fin_step")
        min_ready = sem("min_ready")
        en_ready = sem("en_ready")
        res_ready = sem("res_ready")
        gen_col = sem("gen_col")
        gen_row = sem("gen_row")
        gen_s2 = sem("gen_s2")
        gen_adj = sem("gen_adj")
        gen_step = sem("gen_step")
        gen_scores = sem("gen_scores")
        gen_probs = sem("gen_probs")
        gen_turned = sem("gen_turned")
        gen_copied = sem("gen_copied")
        gen_num = sem("gen_num")
        gen_min = sem("gen_min")
        gen_exp = sem("gen_exp")
        gen_res = sem("gen_res")
        gen_out = sem("gen_out")

        block = ctx.enter_context(nc.Block())

        def chosen(eng):
            eng.wait_ge(flag_ready, 1)
            return eng.value_load(flag[0:1, 0:1], min_val=0, max_val=1)

        @block.sync
        def _(sp):
            for c in range(C):
                sp.dma_start(xs[:, c * CT:(c + 1) * CT, :], x_v[:, c * CT:(c + 1) * CT, :]).then_inc(x_in[c], 16)
            for k in range(R):
                sp.dma_start(ring[:, k, :], adjT[k]).then_inc(adj_in[k], 16)
            general = chosen(sp)
            with sp.If(general == 0):
                with sp.Fori(1, S * Q // R) as r:
                    for k in range(R):
                        sp.wait_ge(mask_ready, r * R + (k - R + 1))
                        sp.dma_start(ring[:, k, :], adjT[r * R + k]).then_inc(adj_in[k], 16)
            with sp.If(general == 1):
                for k in range(R):
                    sp.wait_ge(adj_in[k], 16)
                sp.dma_start(row_adj, adj_v[0]).then_inc(gen_adj, 16)
                with sp.Fori(1, T) as t:
                    sp.wait_ge(gen_scores, t)
                    sp.dma_start(row_adj, adj_v[t]).then_inc(gen_adj, 16)

        @block.gpsimd
        def _(pool):
            nc.gpsimd.memset(ident[:, :], 0.0).then_inc(ident_zero, 1)
            pool.wait_ge(ident_zero, 1)
            nc.gpsimd.affine_select(out=ident[:, :], in_=ident[:, :], compare_op=ALU.not_equal, fill=1.0,
                                    base=0, pattern=[[-1, P]], channel_multiplier=1).then_inc(ident_ready, 1)
            nc.gpsimd.memset(ones[:, :], 1.0)
            nc.gpsimd.memset(tiny[:, :], TINY / 32)
            nc.gpsimd.memset(hsum[:, F:D], float(N)).then_inc(ones_ready, 1)
            for g in range(G):
                pool.wait_ge(rstd_ready, g // 2 + 1)
                if g >= XN:
                    pool.wait_ge(xT_ready, g - XN + 1)
                for k in range(GT - 1):
                    t = g * GT + k
                    last = nc.gpsimd.tensor_scalar(xn[:, g % XN, k, :], xs[:, t, :], mv[:, t, 0:1],
                                                   rstd[:, t:t + 1], ALU.subtract, ALU.mult)
                last.then_inc(xn_pool, 1)

            def g_unit(u):
                if u >= 2:
                    pool.wait_ge(g_ready, u - 1)
                for k in range(GT):
                    t = u * GT + k
                    last = nc.gpsimd.tensor_scalar(gf[:, u % 2, k, :], hs[:, t, 0:D], vf[:, t:t + 1], GSCALE,
                                                   ALU.mult, ALU.mult)
                last.then_inc(gf_ready, 1)
                pool.wait_ge(g_hi, u + 1)
                nc.gpsimd.tensor_tensor(gs[:, u * GT:(u + 1) * GT, D:2 * D], gf[:, u % 2, :, :],
                                        gs[:, u * GT:(u + 1) * GT, 0:D], ALU.subtract).then_inc(g_ready, 1)

            pool.wait_ge(v_ready, 1)
            pool.wait_ge(cq_ready, 1)
            g_unit(0)
            general = chosen(pool)
            with pool.If(general == 0):
                for u in range(1, G):
                    g_unit(u)
                pool.wait_ge(hsum_ready, 1)
                steps = [0]

                def step(ins):
                    steps[0] += 1
                    ins.then_inc(pool_step, 1)
                    pool.wait_ge(pool_step, steps[0])

                step(nc.gpsimd.tensor_copy(hsum_part[:, 0, :], hsum[:, :]))
                step(nc.gpsimd.tensor_tensor(rest[:, :], hsum[:, :], hsum_part[:, 0, :], ALU.subtract))
                step(nc.gpsimd.tensor_copy(hsum_part[:, 1, :], rest[:, :]))
                step(nc.gpsimd.tensor_tensor(rest[:, :], rest[:, :], hsum_part[:, 1, :], ALU.subtract))
                step(nc.gpsimd.tensor_copy(hsum_part[:, 2, :], rest[:, :]))
                for k in range(3):
                    last = nc.gpsimd.tensor_copy(hsum_rows[32 * k:32 * k + 32, :], hsum_part[32 * k:32 * k + 32, k, :])
                last.then_inc(hrows_ready, 1)
                with pool.Fori(0, S) as s:
                    pool.wait_ge(res_ready, s + 1)
                    pool.dma_start(out_v[:, bass.ds(s * ST, ST), :], res[:, :, :]).then_inc(out_done, 16)
                pool.wait_ge(out_done, 16 * S)
            with pool.If(general == 1):
                with pool.Fori(0, T) as t:
                    pool.wait_ge(gen_res, t + 1)
                    pool.dma_start(out_v[:, bass.ds(t, 1), :], g_res.unsqueeze(1)).then_inc(gen_out, 16)
                pool.wait_ge(gen_out, 16 * T)

        @block.tensor
        def _(pe):
            def turn(g):
                pe.wait_ge(xn_pool, g + 1)
                pe.wait_ge(xn_dve, g + 1)
                if g >= 2:
                    pe.wait_ge(yT_ready, g - 1)
                for k in range(GT):
                    last = nc.tensor.transpose(ps[:, g % 2, k * P:(k + 1) * P], xn[:, g % XN, k, :], ident[:, :])
                last.then_inc(xT_ready, 1)

            pe.wait_ge(w_in, 48)
            nc.tensor.matmul(ps[:, 7, 0:2], wT_sb[:, :], a_sb[:, :], start=True, stop=True).then_inc(wa_mm, 1)
            pe.wait_ge(ident_ready, 1)
            turn(0)
            pe.wait_ge(ww_ready, 1)
            for g in range(G):
                if g + 1 < G:
                    turn(g + 1)
                pe.wait_ge(yT_ready, g + 1)
                if g >= 2:
                    pe.wait_ge(h_ready, g - 1)
                for k in range(GT):
                    last = nc.tensor.matmul(ps[:, 2 + 2 * (g % 2) + k // 2, (k % 2) * 256:(k % 2) * 256 + F + 2],
                                            yT[:, g % 2, k * P:(k + 1) * P], ww[:, :], start=True, stop=True)
                last.then_inc(h_mm, 1)
            pe.wait_ge(st_ready, 1)
            pe.wait_ge(norm_ready, 1)
            nc.tensor.transpose(ps[0:4, 0, 0:P], st[:, :], ident[:, :]).then_inc(st_t, 1)
            pe.wait_ge(diag_ready, 1)
            pe.wait_ge(ones_ready, 1)
            nc.tensor.matmul(ps[:, 6, 0:4], ones[0:4, :], diag[:, :], start=True, stop=True).then_inc(mx_mm, 1)
            pe.wait_ge(cq_ready, 1)
            pe.wait_ge(h_ready, G)
            pe.wait_ge(bias_ready, 1)
            for g in range(G):
                for k in range(GT):
                    t = g * GT + k
                    last = nc.tensor.transpose(ps[:, g, k * P:(k + 1) * P], cqp[:, 0, t:t + 1].to_broadcast([P, P]),
                                               ident[:, :])
                last.then_inc(c_turned, 1)
            pe.wait_ge(ysum_ready, 1)
            pe.wait_ge(c_dve, 1)
            nc.tensor.matmul(ps[:, 0, 0:F], square[:, :], ww[:, 0:F], start=True, stop=True).then_inc(hsum_mm, 1)
            pe.wait_ge(hsum_ready, 1)
            pe.wait_ge(c_dve, 2)
            pe.wait_ge(c_act, 6)

            def super_tile(s, first):
                for jb in range(T):
                    if first and jb % GT == 0:
                        pe.wait_ge(g_ready, jb // GT + 1)
                    if first and jb == T - 1:
                        pe.wait_ge(hrows_ready, 1)
                    pe.wait_ge(w_ready, s * T + (jb + 1))
                    for i in range(ST):
                        if jb == 0 and not first and i % HB == 0:
                            pe.wait_ge(acc_ready, (s - 1) * 2 + (i // HB + 1))
                        hi = w16[jb % WR][:, i * P:(i + 1) * P, 1]
                        lo = w16[jb % WR][:, i * P:(i + 1) * P, 0]
                        nc.tensor.matmul(ps[:, i, 0:2 * D], hi, gs[:, jb, :], start=(jb == 0), stop=False)
                        if jb == T - 1:
                            nc.tensor.matmul(ps[:, i, 0:D], tiny[:, :], hsum_rows[:, :], start=False, stop=False)
                        last = nc.tensor.matmul(ps[:, i, 0:D], lo, gs[:, jb, 0:D], start=False,
                                                stop=(jb == T - 1))
                        if jb == T - 1 and i % HB == HB - 1:
                            last.then_inc(acc_done, 1)
                    if jb < T - 1:
                        last.then_inc(w_used, 1)

            general = chosen(pe)
            with pe.If(general == 0):
                super_tile(0, True)
                with pe.Fori(1, S) as s:
                    super_tile(s, False)
            with pe.If(general == 1):
                with pe.Fori(0, T) as t:
                    pe.wait_ge(gen_col, t + 1)
                    nc.tensor.matmul(ps[:, 0, 0:P], square[:, :], ident[:, :], start=True, stop=True).then_inc(gen_row, 1)
                with pe.Fori(0, T) as t:
                    pe.wait_ge(gen_probs, t + 1)
                    for g in range(G):
                        for k in range(GT):
                            last = nc.tensor.transpose(ps[:, 0, k * P:(k + 1) * P], scores_t[:, g * GT + k, :],
                                                       ident[:, :])
                        last.then_inc(gen_turned, 1)
                        pe.wait_ge(gen_copied, t * G + (g + 1))
                        for k in range(GT):
                            j = g * GT + k
                            last = nc.tensor.matmul(ps[:, 1, 0:F], probs_T[:, k * P:(k + 1) * P], hs[:, j, 0:F],
                                                    start=(j == 0), stop=(j == T - 1))
                    last.then_inc(gen_num, 1)

        @block.scalar
        def _(act):
            act.dma_start(wT_sb[:, :], wT).then_inc(w_in, 16)
            act.dma_start(ww[:, 0:F], W).then_inc(w_in, 16)
            act.dma_start(a_sb[:, :], a).then_inc(w_in, 16)

            def deviations(c):
                act.wait_ge(var_ready, c + 1)
                nc.scalar.activation(std[:, c * CT:(c + 1) * CT], mv[:, c * CT:(c + 1) * CT, 1], ACT.Sqrt,
                                     bias=EPS).then_inc(std_ready, 1)

            def read_h(g):
                act.wait_ge(h_mm, g + 1)
                v = ps[:, 2 + 2 * (g % 2):4 + 2 * (g % 2), :].rearrange("p b (k c) -> p (b k) c", k=2)
                nc.scalar.copy(hs[:, g * GT:(g + 1) * GT, :], v[:, :, 0:F + 2]).then_inc(h_ready, 1)

            deviations(0)
            act.wait_ge(w_in, 48)
            nc.scalar.activation(square[:, :], wT_sb[:, :], ACT.Square, accum_out=st[:, 3:4]).then_inc(norm_ready, 1)
            deviations(1)
            for g in range(G):
                act.wait_ge(xT_ready, g + 1)
                if g >= 2:
                    act.wait_ge(h_mm, g - 1)
                nc.scalar.activation(yT[:, g % 2, :], ps[:, g % 2, :], ACT.Relu,
                                     accum_out=ysum[:, g:g + 1]).then_inc(yT_ready, 1)
                if g % 2 == 0 and g // 2 + 2 < C:
                    deviations(g // 2 + 2)
                if g == 4:
                    nc.scalar.activation(m5[0:1, :], std[0:1, 0:1], ACT.Exp, scale=0.0)
                if g >= 1:
                    read_h(g - 1)
            read_h(G - 1)
            act.wait_ge(bias_ready, 1)
            nc.scalar.activation(cqf[:, 0, :], sc[:, :, 0], ACT.Exp, bias=bias_cq[:, :], scale=1.0 - SLOPE)
            nc.scalar.activation(cqf[:, 1, :], sc[:, :, 1], ACT.Exp, bias=bias_cq[:, :],
                                 scale=SLOPE - 1.0).then_inc(act_step, 1)
            act.wait_ge(act_step, 1)
            nc.scalar.mul(cqp16[:, :, :, 1], cqf[:, :, :], TRUNC).then_inc(cq_hi, 1)
            nc.scalar.activation(vf[:, :], sc[:, :, 1], ACT.Exp, bias=neg_m2[:, :]).then_inc(v_ready, 1)

            def g_high(u):
                act.wait_ge(gf_ready, u + 1)
                nc.scalar.copy(gs[:, u * GT:(u + 1) * GT, 0:D], gf[:, u % 2, :, :]).then_inc(g_hi, 1)

            def sanitise(s, q, first):
                act.wait_ge(adj_in[q % R], 16 * (s * (Q // R) + (q // R + 1)))
                if not (first and q < MR):
                    act.wait_ge(w_ready, (s * Q + (q - MR + 1)) * PB)
                nc.scalar.activation(mask[:, q % MR, :], ring[:, q % R, :], ACT.Relu,
                                     scale=LIFT).then_inc(mask_ready, 1)

            for g in range(1, G):
                act.wait_ge(c_turned, g + 1)
                if g < 7:
                    nc.scalar.copy(cp[:, g * GC:(g + 1) * GC], ps[:, g, :]).then_inc(c_act, 1)
                if g == 1:
                    g_high(0)

            def copy_high(s):
                for half in range(2):
                    act.wait_ge(acc_done, s * 2 + (half + 1))
                    b = half * HB
                    nc.scalar.copy(acc[:, b:b + HB, :], ps[:, b:b + HB, 0:D]).then_inc(hi_copied, 1)

            def exponential(s):
                act.wait_ge(min_ready, s + 1)
                nc.scalar.activation(en[:, :, :], en[:, :, :], ACT.Exp).then_inc(en_ready, 1)

            def pieces(s, first):
                for q in range(Q):
                    if first and q % 2 == 1 and q // 2 + 1 < G:
                        g_high(q // 2 + 1)
                    sanitise(s, q, first)
                    if q == 1 and not first:
                        copy_high(s - 1)
                    if q == 4 and not first:
                        exponential(s - 1)

            general = chosen(act)
            with act.If(general == 0):
                pieces(0, True)
                with act.Fori(1, S) as s:
                    pieces(s, False)
                copy_high(S - 1)
                exponential(S - 1)
            with act.If(general == 1):
                with act.Fori(0, T) as t:
                    act.wait_ge(gen_scores, t + 1)
                    nc.scalar.activation(scores, scores, ACT.Exp, bias=neg_max, accum_out=den).then_inc(gen_probs, 1)
                    for g in range(G):
                        act.wait_ge(gen_turned, t * G + (g + 1))
                        nc.scalar.copy(probs_T, ps[:, 0, :]).then_inc(gen_copied, 1)
                    act.wait_ge(gen_min, t + 1)
                    nc.scalar.activation(g_en, g_en, ACT.Exp).then_inc(gen_exp, 1)

        @block.vector
        def _(dve):
            steps = [0]

            def step(ins):
                steps[0] += 1
                ins.then_inc(dve_step, 1)
                dve.wait_ge(dve_step, steps[0])

            def stats(c):
                dve.wait_ge(x_in[c], 16)
                for t in range(c * CT, (c + 1) * CT):
                    last = nc.vector.bn_stats(bst[:, t, :], xs[:, t, :])
                step(last)
                for t in range(c * CT, (c + 1) * CT):
                    last = nc.vector.bn_aggr(mv[:, t, :], bst[:, t, :])
                last.then_inc(var_ready, 1)

            def normalise(c):
                dve.wait_ge(std_ready, c + 1)
                nc.vector.reciprocal(rstd[:, c * CT:(c + 1) * CT], std[:, c * CT:(c + 1) * CT]).then_inc(rstd_ready, 1)
                dve.wait_ge(rstd_ready, c + 1)
                for g in (2 * c, 2 * c + 1):
                    if g >= XN:
                        dve.wait_ge(xT_ready, g - XN + 1)
                    t = g * GT + GT - 1
                    nc.vector.tensor_scalar(xn[:, g % XN, GT - 1, :], xs[:, t, :], mv[:, t, 0:1],
                                            rstd[:, t:t + 1], ALU.subtract, ALU.mult).then_inc(xn_dve, 1)

            stats(0)
            stats(1)
            normalise(0)
            dve.wait_ge(wa_mm, 1)
            nc.vector.tensor_copy(ww[:, F:F + 2], ps[:, 7, 0:2]).then_inc(ww_ready, 1)
            stats(2)
            normalise(1)
            stats(3)
            normalise(2)
            normalise(3)
            dve.wait_ge(h_ready, G)
            nc.vector.tensor_copy(sc[:, :, :], hs[:, :, F:F + 2])
            nc.vector.reduce_max(st[:, 0:2], hs[:, :, F:F + 2].rearrange("p t c -> p c t"), AX.X)
            step(nc.vector.tensor_reduce(m5[:, :], hs[:, :, F + 1], AX.X, ALU.min))
            nc.vector.tensor_scalar(st[:, 2:3], m5[:, :], -1.0, None, ALU.mult).then_inc(st_ready, 1)
            nc.vector.memset(hs[:, :, F:D], 1.0)
            dve.wait_ge(st_t, 1)
            step(nc.vector.reduce_max(m5[0:4, :], ps[0:4, 0, 0:P], AX.X))
            nc.vector.tensor_scalar(diag[:, :], ident[0:4, 0:4], m5[0:4, :], None, ALU.mult).then_inc(diag_ready, 1)
            dve.wait_ge(mx_mm, 1)
            step(nc.vector.tensor_copy(mx[:, :], ps[:, 6, 0:4]))
            step(nc.vector.tensor_tensor(viol[:, 0:1], mx[:, 0:1], mx[:, 2:3], ALU.max))
            nc.vector.tensor_scalar(bias_cq[:, :], viol[:, 0:1], SLOPE - 1.0, LOGTOP, ALU.mult, ALU.add)
            nc.vector.tensor_scalar(neg_m2[:, :], mx[:, 1:2], -1.0, None, ALU.mult).then_inc(bias_ready, 1)
            step(nc.vector.tensor_tensor(viol[:, 1:2], viol[:, 0:1], mx[:, 1:2], ALU.add))
            nc.vector.tensor_scalar(viol[:, 1:2], viol[:, 1:2], 1.0 - SLOPE, -WINDOW, ALU.mult, ALU.add)
            nc.vector.tensor_scalar(viol[:, 2:3], mx[:, 3:4], -NORM2_MAX, None, ALU.add)
            step(nc.vector.tensor_scalar(viol[:, 3:4], mx[:, 3:4], -1.0, NORM2_MIN, ALU.mult, ALU.add))
            dve.wait_ge(cq_hi, 1)
            nc.vector.tensor_tensor(cqp16[:, :, :, 0], cqf[:, :, :], cqp16[:, :, :, 1], ALU.subtract).then_inc(cq_ready, 1)
            step(nc.vector.reduce_max(m5[:, :], viol[:, 1:4], AX.X))
            nc.vector.tensor_scalar(flag[:, :], m5[:, :], 0.0, None, ALU.is_gt).then_inc(flag_ready, 1)
            step(nc.vector.reduce_sum(ysum[:, G:G + 1], ysum[:, 0:G], AX.X))
            nc.vector.tensor_copy(square[:, :], ysum[:, G:G + 1].to_broadcast([P, P])).then_inc(ysum_ready, 1)
            dve.wait_ge(c_turned, 1)
            nc.vector.tensor_copy(cp[:, 0:GC], ps[:, 0, :]).then_inc(c_dve, 1)
            dve.wait_ge(hsum_mm, 1)
            dve.wait_ge(ones_ready, 1)
            nc.vector.tensor_copy(hsum[:, 0:F], ps[:, 0, 0:F]).then_inc(hsum_ready, 1)
            dve.wait_ge(c_turned, G)
            nc.vector.tensor_copy(cp[:, (G - 1) * GC:G * GC], ps[:, G - 1, :]).then_inc(c_dve, 1)
            dve.wait_ge(c_act, 1)

            def weights(s, jb, first):
                q = jb // PB
                if jb % PB == 0:
                    dve.wait_ge(mask_ready, s * Q + (q + 1))
                if jb >= WR:
                    dve.wait_ge(w_used, s * (T - 1) + (jb - WR + 1))
                elif not first and jb < WR - 1:
                    dve.wait_ge(w_used, (s - 1) * (T - 1) + (T - WR + jb + 1))
                elif not first:
                    dve.wait_ge(acc_done, s * 2)
                nc.vector.scalar_tensor_tensor(
                    w[:, jb % WR, :], cp[:, bass.ds(s * SC, SC)], cqp[:, 1, jb:jb + 1],
                    mask[:, q % MR, (jb % PB) * SC:(jb % PB + 1) * SC], ALU.max, ALU.min).then_inc(w_ready, 1)

            def add_low(s):
                for half in range(2):
                    dve.wait_ge(hi_copied, s * 2 + (half + 1))
                    b = half * HB
                    nc.vector.tensor_tensor(acc[:, b:b + HB, :], acc[:, b:b + HB, :], ps[:, b:b + HB, D:2 * D],
                                            ALU.add).then_inc(acc_ready, 1)
                dve.wait_ge(acc_ready, s * 2 + 2)
                nc.vector.reciprocal(rt[:, :], acc[:, :, F]).then_inc(fin_step, 1)
                dve.wait_ge(fin_step, s * 3 + 1)
                nc.vector.tensor_tensor(acc[:, :, 0:F], acc[:, :, 0:F], rt[:, :].unsqueeze(2).to_broadcast([P, ST, F]),
                                        ALU.mult).then_inc(fin_step, 1)
                dve.wait_ge(fin_step, s * 3 + 2)
                nc.vector.tensor_scalar(en[:, :, :], acc[:, :, 0:F], 0.0, None, ALU.min).then_inc(min_ready, 1)

            def finish(s):
                dve.wait_ge(en_ready, s + 1)
                nc.vector.scalar_tensor_tensor(acc[:, :, 0:F], acc[:, :, 0:F], 0.0, en[:, :, :], ALU.max,
                                               ALU.add).then_inc(fin_step, 1)
                dve.wait_ge(fin_step, s * 3 + 3)
                nc.vector.scalar_tensor_tensor(res[:, :, :], acc[:, :, 0:F], -1.0, xs[:, bass.ds(s * ST, ST), :],
                                               ALU.add, ALU.add).then_inc(res_ready, 1)

            def blocks(s, first):
                for jb in range(T):
                    weights(s, jb, first)
                    if not first and jb == 2:
                        add_low(s - 1)
                    if not first and jb == 12:
                        finish(s - 1)
                if not first:
                    dve.wait_ge(out_done, 16 * s)

            general = chosen(dve)
            with dve.If(general == 0):
                blocks(0, True)
                with dve.Fori(1, S) as s:
                    blocks(s, False)
                add_low(S - 1)
                finish(S - 1)
            with dve.If(general == 1):
                with dve.Fori(0, T) as t:
                    nc.vector.tensor_copy(square[:, :], sc[:, bass.ds(t, 1), 1].to_broadcast([P, P])).then_inc(gen_col, 1)
                    dve.wait_ge(gen_row, t + 1)
                    nc.vector.tensor_copy(s2_bc_t[:, bass.ds(t, 1), :],
                                          ps[:, 0, 0:P].unsqueeze(1)).then_inc(gen_s2, 1)
                    dve.wait_ge(gen_s2, t + 1)
                STEPS = 7

                def row_tile(t, first):
                    done = [0]

                    def gstep(ins):
                        done[0] += 1
                        ins.then_inc(gen_step, 1)
                        dve.wait_ge(gen_step, t * STEPS + done[0])

                    dve.wait_ge(gen_adj, 16 * (t + 1))
                    nc.vector.tensor_scalar(penalty, row_adj, 0.0, NEG, ALU.is_le, ALU.mult)
                    gstep(nc.vector.tensor_scalar(scores, s2_bc, sc[:, bass.ds(t, 1), 0], None, ALU.add))
                    gstep(nc.vector.scalar_tensor_tensor(scores, scores, SLOPE, scores, ALU.mult, ALU.max))
                    gstep(nc.vector.tensor_tensor(scores, scores, penalty, ALU.add))
                    gstep(nc.vector.reduce_max(g_cols[:, 2:3], scores, AX.X))
                    nc.vector.tensor_scalar(neg_max, g_cols[:, 2:3], -1.0, None, ALU.mult).then_inc(gen_scores, 1)
                    dve.wait_ge(gen_probs, t + 1)
                    gstep(nc.vector.reciprocal(g_cols[:, 3:4], den))
                    dve.wait_ge(gen_num, t + 1)
                    if not first:
                        dve.wait_ge(gen_out, 16 * t)
                    gstep(nc.vector.tensor_scalar(g_hp, ps[:, 1, 0:F], g_cols[:, 3:4], None, ALU.mult))
                    nc.vector.tensor_scalar(g_en, g_hp, 0.0, None, ALU.min).then_inc(gen_min, 1)
                    dve.wait_ge(gen_exp, t + 1)
                    gstep(nc.vector.scalar_tensor_tensor(g_hp, g_hp, 0.0, g_en, ALU.max, ALU.add))
                    nc.vector.scalar_tensor_tensor(g_res.unsqueeze(1), g_hp.unsqueeze(1), -1.0,
                                                   xs[:, bass.ds(t, 1), :], ALU.add, ALU.add).then_inc(gen_res, 1)

                row_tile(0, True)
                with dve.Fori(1, T) as t:
                    row_tile(t, False)

    return nc


def kernel(x, adj, L0_gnn_W, L0_gnn_a):
    import numpy as _np
    import concourse.bacc as _bacc
    from concourse import mybir as _mybir
    from concourse.bass_utils import run_bass_kernel_spmd as _run

    nc = _bacc.Bacc("TRN2", target_bir_lowering=False, num_devices=1)
    x, adj, W, a = (_np.asarray(v) for v in (x, adj, L0_gnn_W, L0_gnn_a))
    blocks = adj.reshape(128, 4, 8, 128, 16, 2).transpose(1, 4, 3, 5, 2, 0).reshape(64, 128, 2048)
    arrays = {
        "x": _np.ascontiguousarray(x),
        "adj": _np.ascontiguousarray(adj),
        "adjT": _np.ascontiguousarray(blocks),
        "W": _np.ascontiguousarray(W),
        "wT": _np.ascontiguousarray(W.T),
        "a": _np.ascontiguousarray(a.reshape(2, 128).T),
    }
    args = [nc.dram_tensor(f"in_{n}", v.shape, _mybir.dt.from_np(v.dtype), kind="ExternalInput").ap()
            for n, v in arrays.items()]
    args.append(nc.dram_tensor("out", x.shape, _mybir.dt.float32, kind="ExternalOutput").ap())
    gat_kernel(nc, *args)
    r = _run(nc, [{f"in_{n}": v for n, v in arrays.items()}], core_ids=[0])
    return r.results[0]["out"]
```

```python
import concourse.bass as bass
from concourse import mybir
from contextlib import ExitStack


def gat_kernel(nc: bass.Bass, x: bass.AP, adj: bass.AP, adjT: bass.AP, W: bass.AP, wT: bass.AP, a: bass.AP,
               out: bass.AP):
    import math

    fp32 = mybir.dt.float32
    fp16 = mybir.dt.float16
    bf16 = mybir.dt.bfloat16
    i32 = mybir.dt.int32
    ALU = mybir.AluOpType
    ACT = mybir.ActivationFunctionType
    AX = mybir.AxisListType

    P = 128
    N, F = x.shape
    T = N // P
    GT = 4
    G = T // GT
    GC = GT * P
    CT = 8
    C = T // CT
    ST = 8
    S = T // ST
    SC = ST * P
    SH = SC // 2
    HB = ST // 2
    QB = ST // 4
    R = 16
    MR = 8
    WR = 8
    XN = 4
    HA = 4
    D = F + 1
    S1, NS2, S2, HC = F + 1, F + 2, F + 3, F + 4
    EPS = 1e-5
    SLOPE = 0.2
    NEG = -9000000000000000.0
    LIFT = 2.0 ** 96
    LOGTOP = 12 * math.log(2.0)
    GSCALE = 1024.0
    TRUNC = 1.0 - 2.0 ** -11
    GB = 2
    LAST = 4
    WARM = 24
    WARM_A, WARM_B, WARM_C = 10, 4, 16
    WARM_SUM, WARM_TOP, WARM_FACTORS = 10, 4, 16
    EARLY, MORE = 3, 1
    COPY_AT, ELU_AT, ADD_AT, OUT_AT = 5, (9, 11, 13, 15), 2, 20
    TINY = 2.0 ** -80
    TINY_BLOCK = T - LAST - 1
    WINDOW = 6.0
    NORM2_MAX, NORM2_MIN = 30.0, 2.0 ** -8

    x_v = x.rearrange("(p t) f -> p t f", p=P)
    out_v = out.rearrange("(p t) f -> p t f", p=P)
    adj_v = adj.rearrange("(p t) n -> t p n", p=P)

    ctx = ExitStack()
    with ctx:
        def sb(name, shape, dt=fp32):
            return ctx.enter_context(nc.sbuf_tensor(name, shape, dt))

        def sem(name):
            return ctx.enter_context(nc.semaphore(name))

        xs = sb("xs", [P, T, F])
        ww = sb("ww", [P, HC])
        wT_sb = sb("wT_sb", [P, F])
        a_sb = sb("a_sb", [P, 2])
        ident = sb("ident", [P, P])
        bst = sb("bst", [P, T, 6])
        mv = sb("mv", [P, T, 2])
        std = sb("std", [P, T])
        rstd = sb("rstd", [P, T])
        shift = sb("shift", [P, T])
        ysum = sb("ysum", [P, G + 1])
        square = sb("square", [P, P])
        hsum = sb("hsum", [P, D])
        rest = sb("rest", [P, D])
        hsum_part = sb("hsum_part", [P, 3, D], bf16)
        hsum_rows = sb("hsum_rows", [96, D], bf16)
        tiny = sb("tiny", [96, P], bf16)
        hs = sb("hs", [P, T, HC])
        st = sb("st", [P, 3])
        top = sb("top", [3, 1])
        mx = sb("mx", [P, 3])
        bias_cq = sb("bias_cq", [P, 1])
        bias_v = sb("bias_v", [P, 1])
        viol = sb("viol", [P, 4])
        flag = sb("flag", [P, 1], i32)
        cqf = sb("cqf", [P, T, 2])
        cqp = sb("cqp", [P, T, 2])
        vf = sb("vf", [P, T])
        cp = sb("cp", [P, N])
        gf = sb("gf", [P, 2, GT, D])
        gs = sb("gs", [P, T, 2 * D], fp16)
        ring = sb("ring", [P, R, SC], i32)
        mask = sb("mask", [P, MR, SC], bf16)
        w = sb("w", [P, WR, SC])
        xn = w[:, 0:2, :].rearrange("p b (g k f) -> p (b g) k f", g=2, k=GT)
        yT = w[:, 2, :].rearrange("p (g n) -> p g n", g=2)
        acc = sb("acc", [P, ST, D])
        rt = sb("rt", [P, ST])
        res = sb("res", [P, ST, F])
        en = sb("en", [P, ST, F])

        row_adj = ring[:, 0:4, :].rearrange("p k n -> p (k n)")
        scores = w[:, 0:4, :].rearrange("p b n -> p (b n)")
        penalty = ring[:, 4:8, :].rearrange("p k n -> p (k n)").bitcast(fp32)
        scores_t = scores.rearrange("p (q t) -> p t q", t=T)
        s2_bc = cp[:, :]
        s2_bc_t = cp[:, :].rearrange("p (q t) -> p t q", t=T)
        late = w[:, WR - 1, :]
        probs_T = late[:, 0:GC]
        g_hp = late[:, GC:GC + F]
        g_en = late[:, GC + F:GC + 2 * F]
        g_res = late[:, GC + 2 * F:GC + 3 * F]
        g_cols = late[:, GC + 3 * F:GC + 3 * F + 4]
        neg_max, den = g_cols[:, 0:1], g_cols[:, 1:2]

        ps = ctx.enter_context(nc.psum_tensor("ps", [P, 8, 512], fp32))

        cqp16 = cqp[:, :, :].bitcast(fp16).rearrange("p t (c h) -> p t c h", h=2)
        w16 = [w[:, k, :].bitcast(fp16).rearrange("p (n h) -> p n h", h=2) for k in range(WR)]

        x_in = [sem(f"x_in{c}") for c in range(C)]
        w_in = sem("w_in")
        adj_in = [sem(f"adj_in{k}") for k in range(R)]
        out_done = sem("out_done")
        last_out = sem("last_out")
        ident_zero = sem("ident_zero")
        ident_ready = sem("ident_ready")
        consts_ready = sem("consts_ready")
        wa_mm = sem("wa_mm")
        ww_ready = sem("ww_ready")
        norm_ready = sem("norm_ready")
        stats_step = sem("stats_step")
        var_ready = sem("var_ready")
        std_ready = sem("std_ready")
        scale_ready = sem("scale_ready")
        xn_pool = sem("xn_pool")
        xn_dve = sem("xn_dve")
        xT_ready = sem("xT_ready")
        yT_ready = sem("yT_ready")
        h_mm = sem("h_mm")
        h_act = sem("h_act")
        h_dve = sem("h_dve")
        less_one = sem("less_one")
        ysum_ready = sem("ysum_ready")
        hsum_mm = sem("hsum_mm")
        hsum_ready = sem("hsum_ready")
        hsum_step = sem("hsum_step")
        hrows_ready = sem("hrows_ready")
        st_ready = sem("st_ready")
        st_turned = sem("st_turned")
        top_ready = sem("top_ready")
        mx_mm = sem("mx_mm")
        bias_ready = sem("bias_ready")
        mx_ready = sem("mx_ready")
        ones_col = sem("ones_col")
        dve_step = sem("dve_step")
        flag_ready = sem("flag_ready")
        cq_exp = sem("cq_exp")
        cq_hi = sem("cq_hi")
        cq_ready = sem("cq_ready")
        v_ready = sem("v_ready")
        c_turned = sem("c_turned")
        c_act = sem("c_act")
        c_dve = sem("c_dve")
        gf_ready = sem("gf_ready")
        g_hi = sem("g_hi")
        g_ready = sem("g_ready")
        mask_ready = sem("mask_ready")
        w_ready = sem("w_ready")
        mask_half = sem("mask_half")
        w_half = sem("w_half")
        w_used = sem("w_used")
        acc_done = sem("acc_done")
        hi_copied = sem("hi_copied")
        acc_ready = sem("acc_ready")
        rt_ready = sem("rt_ready")
        exp_ready = sem("exp_ready")
        relu_ready = sem("relu_ready")
        relu_x = sem("relu_x")
        acc_free = sem("acc_free")
        last_relu = sem("last_relu")
        last_res = sem("last_res")
        gen_col = sem("gen_col")
        gen_row = sem("gen_row")
        gen_s2 = sem("gen_s2")
        gen_adj = sem("gen_adj")
        gen_step = sem("gen_step")
        gen_scores = sem("gen_scores")
        gen_probs = sem("gen_probs")
        gen_turned = sem("gen_turned")
        gen_copied = sem("gen_copied")
        gen_num = sem("gen_num")
        gen_min = sem("gen_min")
        gen_exp = sem("gen_exp")
        gen_res = sem("gen_res")
        gen_out = sem("gen_out")

        G_UNITS = [(0, 2), (2, 4)] + [(t, t + GT) for t in range(GT, T, GT)]
        UNITS_FOR = [1 + [t for t, _ in G_UNITS].index(jb) if jb in [t for t, _ in G_UNITS] else 0 for jb in range(T)]
        HIGH_AFTER = [EARLY, EARLY + 2] + [4 * u - 5 for u in range(3, len(G_UNITS))]
        C_DVE = (0, 2)
        C_ACT = tuple(g for g in range(G) if g not in C_DVE)
        DVE_TILES = [1] * (G - 2) + [2, 2]

        block = ctx.enter_context(nc.Block())

        def chosen(eng):
            eng.wait_ge(flag_ready, 1)
            return eng.value_load(flag[0:1, 0:1], min_val=0, max_val=1)

        @block.sync
        def _(sp):
            for c in range(C):
                sp.dma_start(xs[:, c * CT:(c + 1) * CT, :], x_v[:, c * CT:(c + 1) * CT, :]).then_inc(x_in[c], 16)

            for k in range(R):
                sp.dma_start(ring[:, k, :], adjT[k]).then_inc(adj_in[k], 16)
            general = chosen(sp)
            with sp.If(general == 0):
                with sp.Fori(1, S * T // R) as r:
                    for k in range(R):
                        sp.wait_ge(mask_ready, r * R + (k - R + 1))
                        sp.dma_start(ring[:, k, :], adjT[r * R + k]).then_inc(adj_in[k], 16)
                for half in range(2):
                    sp.wait_ge(last_res, 2 * half + 2)
                    t = (S - 1) * ST + half * HB
                    sp.dma_start(out_v[:, t:t + HB, :], res[:, half * HB:(half + 1) * HB, :]).then_inc(last_out, 16)
                sp.wait_ge(last_out, 32)
            with sp.If(general == 1):
                for k in range(R):
                    sp.wait_ge(adj_in[k], 16)
                sp.wait_ge(mask_ready, EARLY + MORE)
                sp.dma_start(row_adj, adj_v[0]).then_inc(gen_adj, 16)
                with sp.Fori(1, T) as t:
                    sp.wait_ge(gen_scores, t)
                    sp.dma_start(row_adj, adj_v[t]).then_inc(gen_adj, 16)

        @block.gpsimd
        def _(pool):
            nc.gpsimd.memset(ident[:, :], 0.0).then_inc(ident_zero, 1)
            pool.wait_ge(ident_zero, 1)
            nc.gpsimd.affine_select(out=ident[:, :], in_=ident[:, :], compare_op=ALU.not_equal, fill=1.0,
                                    base=0, pattern=[[-1, P]], channel_multiplier=1).then_inc(ident_ready, 1)
            nc.gpsimd.memset(ww[:, F:F + 1], 0.0)
            nc.gpsimd.memset(hsum[:, F:D], float(N))
            nc.gpsimd.memset(tiny[:, :], TINY / 32).then_inc(consts_ready, 1)
            nc.gpsimd.memset(acc[:, :, F], 1.0).then_inc(acc_free, 1)

            for g in range(G):
                pool.wait_ge(scale_ready, 2 * (g // 2 + 1))
                if g >= XN:
                    pool.wait_ge(xT_ready, g - XN + 1)
                for k in range(GT - DVE_TILES[g]):
                    t = g * GT + k
                    last = nc.gpsimd.tensor_scalar(xn[:, g % XN, k, :], xs[:, t, :], rstd[:, t:t + 1],
                                                   shift[:, t:t + 1], ALU.mult, ALU.add)
                last.then_inc(xn_pool, 1)
            def g_unit(u):
                t0, t1 = G_UNITS[u]
                if u >= 2:
                    pool.wait_ge(g_ready, u - 1)
                for k in range(t1 - t0):
                    t = t0 + k
                    last = nc.gpsimd.tensor_scalar(gf[:, u % 2, k, :], hs[:, t, 0:D], vf[:, t:t + 1], GSCALE,
                                                   ALU.mult, ALU.mult)
                last.then_inc(gf_ready, 1)
                pool.wait_ge(g_hi, u + 1)
                nc.gpsimd.tensor_tensor(gs[:, t0:t1, D:2 * D], gf[:, u % 2, 0:t1 - t0, :], gs[:, t0:t1, 0:D],
                                        ALU.subtract).then_inc(g_ready, 1)

            pool.wait_ge(v_ready, 1)
            pool.wait_ge(ones_col, 1)
            g_unit(0)
            general = chosen(pool)
            with pool.If(general == 0):
                for u in range(1, len(G_UNITS)):
                    g_unit(u)
                pool.wait_ge(hsum_ready, 1)
                steps = [0]

                def step(ins):
                    steps[0] += 1
                    ins.then_inc(hsum_step, 1)
                    pool.wait_ge(hsum_step, steps[0])

                step(nc.gpsimd.tensor_copy(hsum_part[:, 0, :], hsum[:, :]))
                step(nc.gpsimd.tensor_tensor(rest[:, :], hsum[:, :], hsum_part[:, 0, :], ALU.subtract))
                step(nc.gpsimd.tensor_copy(hsum_part[:, 1, :], rest[:, :]))
                step(nc.gpsimd.tensor_tensor(rest[:, :], rest[:, :], hsum_part[:, 1, :], ALU.subtract))
                step(nc.gpsimd.tensor_copy(hsum_part[:, 2, :], rest[:, :]))
                for k in range(3):
                    last = nc.gpsimd.tensor_copy(hsum_rows[32 * k:32 * k + 32, :], hsum_part[32 * k:32 * k + 32, k, :])
                last.then_inc(hrows_ready, 1)
                pool.wait_ge(less_one, C)
                with pool.Fori(0, S - 1) as s:
                    pool.wait_ge(relu_ready, s + 1)
                    nc.gpsimd.tensor_tensor(res[:, :, :], acc[:, :, 0:F], xs[:, bass.ds(s * ST, ST), :],
                                            ALU.add).then_inc(relu_x, 1)
                    pool.wait_ge(acc_free, s + 2)
                    pool.dma_start(out_v[:, bass.ds((s + 1) * ST - ST, ST), :], res[:, :, :]).then_inc(out_done, 16)
                    pool.wait_ge(out_done, s * 16 + 16)
                for k in range(4):
                    b = slice(k * QB, (k + 1) * QB)
                    pool.wait_ge(last_relu, k + 1)
                    nc.gpsimd.tensor_tensor(res[:, b, :], res[:, b, :],
                                            xs[:, (S - 1) * ST + k * QB:(S - 1) * ST + (k + 1) * QB, :],
                                            ALU.add).then_inc(relu_x, 1)
            with pool.If(general == 1):
                with pool.Fori(0, T) as t:
                    pool.wait_ge(gen_res, t + 1)
                    pool.dma_start(out_v[:, bass.ds(t, 1), :], g_res.unsqueeze(1)).then_inc(gen_out, 16)
                pool.wait_ge(gen_out, 16 * T)

        @block.tensor
        def _(pe):
            def turn(g):
                pe.wait_ge(xn_pool, g + 1)
                pe.wait_ge(xn_dve, g + 1)
                if g >= 2:
                    pe.wait_ge(yT_ready, g - 1)
                for k in range(GT):
                    last = nc.tensor.transpose(ps[:, g % 2, k * P:(k + 1) * P], xn[:, g % XN, k, :], ident[:, :])
                last.then_inc(xT_ready, 1)

            def keep_warm(bank, n):
                for _ in range(n):
                    nc.tensor.matmul(ps[:, bank, 0:P], tiny[:, :], tiny[:, :], start=True, stop=True)

            pe.wait_ge(ident_ready, 1)
            for k in range(WARM):
                nc.tensor.transpose(ps[:, 7, 0:P], ident[:, :], ident[:, :])
            pe.wait_ge(w_in, 48)
            nc.tensor.matmul(ps[:, 7, 0:2], wT_sb[:, :], a_sb[:, :], start=True, stop=True).then_inc(wa_mm, 1)
            turn(0)
            pe.wait_ge(ww_ready, 1)
            for g in range(G):
                if g + 1 < G:
                    turn(g + 1)
                pe.wait_ge(yT_ready, g + 1)
                if 2 <= g < HA + 2:
                    pe.wait_ge(h_act, g - 1)
                elif g >= HA + 2:
                    pe.wait_ge(h_dve, g - HA - 1)
                for k in range(GT):
                    last = nc.tensor.matmul(ps[:, 2 + 2 * (g % 2) + k // 2, (k % 2) * 256:(k % 2) * 256 + HC],
                                            yT[:, g % 2, k * P:(k + 1) * P], ww[:, :], start=True, stop=True)
                last.then_inc(h_mm, 1)
            pe.wait_ge(ysum_ready, 1)
            nc.tensor.matmul(ps[:, 0, 0:F], square[:, :], ww[:, 0:F], start=True, stop=True).then_inc(hsum_mm, 1)
            pe.wait_ge(consts_ready, 1)
            pe.wait_ge(h_dve, G - HA - 1)
            keep_warm(2, WARM_SUM)
            pe.wait_ge(st_ready, 1)
            pe.wait_ge(norm_ready, 1)
            nc.tensor.transpose(ps[0:3, 6, 0:P], st[:, :], ident[:, :]).then_inc(st_turned, 1)
            keep_warm(2, WARM_TOP)
            pe.wait_ge(top_ready, 1)
            nc.tensor.matmul(ps[:, 7, 0:3], top[:, :].to_broadcast([3, P]), ident[0:3, 0:3], start=True,
                             stop=True).then_inc(mx_mm, 1)
            keep_warm(2, WARM_FACTORS)
            pe.wait_ge(cq_ready, 1)
            pe.wait_ge(h_dve, G - HA)
            pe.wait_ge(hsum_ready, 1)
            pe.wait_ge(mx_ready, 1)
            for g in range(G):
                for k in range(GT):
                    t = g * GT + k
                    last = nc.tensor.transpose(ps[:, g, k * P:(k + 1) * P], cqp[:, t, 0:1].to_broadcast([P, P]),
                                               ident[:, :])
                last.then_inc(c_turned, 1)

            def products(s, first, jb, banks):
                if banks[0] == 0:
                    if first and UNITS_FOR[jb]:
                        pe.wait_ge(g_ready, UNITS_FOR[jb])
                    if first and jb == TINY_BLOCK:
                        pe.wait_ge(hrows_ready, 1)
                    if jb == T - 1:
                        pe.wait_ge(w_half, s + 1)
                    else:
                        pe.wait_ge(w_ready, s * T + (jb + 1))
                if banks[0] == HB and jb == T - 1:
                    pe.wait_ge(w_ready, s * T + T)
                for i in banks:
                    hi = w16[jb % WR][:, i * P:(i + 1) * P, 1]
                    lo = w16[jb % WR][:, i * P:(i + 1) * P, 0]
                    nc.tensor.matmul(ps[:, i, 0:2 * D], hi, gs[:, jb, :], start=(jb == 0), stop=False)
                    if jb == TINY_BLOCK:
                        nc.tensor.matmul(ps[:, i, 0:D], tiny[:, :], hsum_rows[:, :], start=False, stop=False)
                    last = nc.tensor.matmul(ps[:, i, 0:D], lo, gs[:, jb, 0:D], start=False, stop=(jb == T - 1))
                if jb == T - 1:
                    last.then_inc(acc_done, 1)
                elif banks[-1] == ST - 1:
                    last.then_inc(w_used, 1)

            def super_tile(s, first):
                for jb in range(0, T - LAST, GB):
                    for half in range(2):
                        if first and jb == 0:
                            pe.wait_ge(c_dve, len([g for g in C_DVE if g // HB <= half]))
                            pe.wait_ge(c_act, len([g for g in C_ACT if g // HB <= half]))
                        if jb == 0 and not first:
                            pe.wait_ge(acc_ready, (s - 1) * 2 + (half + 1))
                        for k in range(GB):
                            products(s, first, jb + k, range(half * HB, (half + 1) * HB))
                for quarter in range(4):
                    for jb in range(T - LAST, T):
                        products(s, first, jb, range(quarter * QB, (quarter + 1) * QB))

            general = chosen(pe)
            with pe.If(general == 0):
                super_tile(0, True)
                with pe.Fori(1, S) as s:
                    super_tile(s, False)
            with pe.If(general == 1):
                pe.wait_ge(c_dve, len(C_DVE))
                pe.wait_ge(c_act, len(C_ACT))
                with pe.Fori(0, T) as t:
                    pe.wait_ge(gen_col, t + 1)
                    nc.tensor.matmul(ps[:, 0, 0:P], square[:, :], ident[:, :], start=True, stop=True).then_inc(gen_row, 1)
                with pe.Fori(0, T) as t:
                    pe.wait_ge(gen_probs, t + 1)
                    for g in range(G):
                        for k in range(GT):
                            last = nc.tensor.transpose(ps[:, 0, k * P:(k + 1) * P], scores_t[:, g * GT + k, :],
                                                       ident[:, :])
                        last.then_inc(gen_turned, 1)
                        pe.wait_ge(gen_copied, t * G + (g + 1))
                        for k in range(GT):
                            j = g * GT + k
                            last = nc.tensor.matmul(ps[:, 1, 0:F], probs_T[:, k * P:(k + 1) * P], hs[:, j, 0:F],
                                                    start=(j == 0), stop=(j == T - 1))
                    last.then_inc(gen_num, 1)

        @block.scalar
        def _(act):
            act.dma_start(wT_sb[:, :], wT).then_inc(w_in, 16)
            act.dma_start(ww[:, 0:F], W).then_inc(w_in, 16)
            act.dma_start(a_sb[:, :], a).then_inc(w_in, 16)

            def deviations(c):
                act.wait_ge(var_ready, c + 1)
                nc.scalar.activation(std[:, c * CT:(c + 1) * CT], mv[:, c * CT:(c + 1) * CT, 1], ACT.Sqrt,
                                     bias=EPS).then_inc(std_ready, 1)

            def read_h(g):
                act.wait_ge(h_mm, g + 1)
                v = ps[:, 2 + 2 * (g % 2):4 + 2 * (g % 2), :].rearrange("p b (k c) -> p (b k) c", k=2)
                nc.scalar.copy(hs[:, g * GT:(g + 1) * GT, :], v[:, :, 0:HC]).then_inc(h_act, 1)

            def sanitise(s, jb, first):
                act.wait_ge(adj_in[jb % R], 16 * (s * (T // R) + (jb // R + 1)))
                if not (first and jb < MR):
                    act.wait_ge(w_ready, s * T + (jb - MR + 1))
                if jb == T - 1:
                    nc.scalar.activation(mask[:, jb % MR, 0:SH], ring[:, jb % R, 0:SH], ACT.Relu,
                                         scale=LIFT).then_inc(mask_half, 1)
                    nc.scalar.activation(mask[:, jb % MR, SH:SC], ring[:, jb % R, SH:SC], ACT.Relu,
                                         scale=LIFT).then_inc(mask_ready, 1)
                else:
                    nc.scalar.activation(mask[:, jb % MR, :], ring[:, jb % R, :], ACT.Relu,
                                         scale=LIFT).then_inc(mask_ready, 1)

            deviations(0)
            act.wait_ge(w_in, 48)
            nc.scalar.activation(square[:, :], wT_sb[:, :], ACT.Square, accum_out=st[:, 2:3]).then_inc(norm_ready, 1)
            for g in range(G):
                if g % 2 == 0 and g // 2 + 1 < C:
                    deviations(g // 2 + 1)
                act.wait_ge(xT_ready, g + 1)
                if g >= 2:
                    act.wait_ge(h_mm, g - 1)
                nc.scalar.activation(yT[:, g % 2, :], ps[:, g % 2, :], ACT.Relu,
                                     accum_out=ysum[:, g:g + 1]).then_inc(yT_ready, 1)
                if 1 <= g <= HA:
                    read_h(g - 1)
            for jb in range(EARLY):
                sanitise(0, jb, True)
            nc.scalar.activation(rt[0:1, 0:1], std[0:1, 0:1], ACT.Exp, scale=0.0)
            act.wait_ge(bias_ready, 1)
            act.wait_ge(h_dve, G - HA)
            nc.scalar.activation(cqf[:, :, :], hs[:, :, S1:S1 + 2], ACT.Exp, bias=bias_cq[:, :],
                                 scale=1.0 - SLOPE).then_inc(cq_exp, 1)
            act.wait_ge(cq_exp, 1)
            nc.scalar.mul(cqp16[:, :, :, 1], cqf[:, :, :], TRUNC).then_inc(cq_hi, 1)
            nc.scalar.activation(vf[:, :], hs[:, :, S2], ACT.Exp, bias=bias_v[:, :]).then_inc(v_ready, 1)

            def g_high(u):
                t0, t1 = G_UNITS[u]
                act.wait_ge(gf_ready, u + 1)
                nc.scalar.copy(gs[:, t0:t1, 0:D], gf[:, u % 2, 0:t1 - t0, :]).then_inc(g_hi, 1)

            for g in C_ACT:
                act.wait_ge(c_turned, g + 1)
                nc.scalar.copy(cp[:, g * GC:(g + 1) * GC], ps[:, g, :]).then_inc(c_act, 1)
                if g == 1:
                    g_high(0)

            for jb in range(EARLY, EARLY + MORE):
                sanitise(0, jb, True)

            def copy_high(s):
                act.wait_ge(acc_free, s + 1)
                for half in range(2):
                    act.wait_ge(acc_done, s * 4 + (2 * half + 2))
                    b = half * HB
                    nc.scalar.copy(acc[:, b:b + HB, :], ps[:, b:b + HB, 0:D]).then_inc(hi_copied, 1)

            def elu_part(s, part):
                if part == 0:
                    act.wait_ge(rt_ready, s + 1)
                if part == 2:
                    act.wait_ge(exp_ready, s + 1)
                for b in range((part % 2) * HB, (part % 2 + 1) * HB):
                    if part < 2:
                        last = nc.scalar.activation(en[:, b, :], acc[:, b, 0:F], ACT.Exp, scale=rt[:, b:b + 1])
                    else:
                        last = nc.scalar.activation(acc[:, b, 0:F], acc[:, b, 0:F], ACT.Relu, scale=rt[:, b:b + 1])
                if part == 1:
                    last.then_inc(exp_ready, 1)
                if part == 3:
                    last.then_inc(relu_ready, 1)

            def masks(s, first):
                for jb in range(EARLY + MORE - 1 if first else 0, T):
                    if not first or jb >= EARLY + MORE:
                        sanitise(s, jb, first)
                    if first and jb in HIGH_AFTER:
                        g_high(HIGH_AFTER.index(jb) + 1)
                    if jb == COPY_AT and not first:
                        copy_high(s - 1)
                    if not first and jb in ELU_AT:
                        elu_part(s - 1, ELU_AT.index(jb))

            general = chosen(act)
            with act.If(general == 0):
                masks(0, True)
                with act.Fori(1, S) as s:
                    masks(s, False)
                act.wait_ge(acc_free, S)
                for k in range(4 + 1):
                    if k < 4:
                        b = slice(k * QB, (k + 1) * QB)
                        act.wait_ge(acc_done, (S - 1) * 4 + k + 1)
                        nc.scalar.copy(acc[:, b, :], ps[:, b, 0:D]).then_inc(hi_copied, 1)
                    if k >= 1:
                        act.wait_ge(rt_ready, (S - 1) + k)
                        for b in range((k - 1) * QB, k * QB):
                            last = nc.scalar.activation(en[:, b, :], acc[:, b, 0:F], ACT.Exp, scale=rt[:, b:b + 1])
                        last.then_inc(exp_ready, 1)
            with act.If(general == 1):
                with act.Fori(0, T) as t:
                    act.wait_ge(gen_scores, t + 1)
                    nc.scalar.activation(scores, scores, ACT.Exp, bias=neg_max, accum_out=den).then_inc(gen_probs, 1)
                    for g in range(G):
                        act.wait_ge(gen_turned, t * G + (g + 1))
                        nc.scalar.copy(probs_T, ps[:, 0, :]).then_inc(gen_copied, 1)
                    act.wait_ge(gen_min, t + 1)
                    nc.scalar.activation(g_en, g_en, ACT.Exp).then_inc(gen_exp, 1)

        @block.vector
        def _(dve):
            steps = [0]

            def step(ins):
                steps[0] += 1
                ins.then_inc(dve_step, 1)
                dve.wait_ge(dve_step, steps[0])

            def moments(t):
                if t % CT == 0:
                    dve.wait_ge(x_in[t // CT], 16)
                nc.vector.bn_stats(bst[:, t, :], xs[:, t, :]).then_inc(stats_step, 1)

            def aggregate(c):
                dve.wait_ge(stats_step, (c + 1) * CT)
                for t in range(c * CT, (c + 1) * CT):
                    last = nc.vector.bn_aggr(mv[:, t, :], bst[:, t, :])
                last.then_inc(var_ready, 1)

            def scales(c):
                cols = slice(c * CT, (c + 1) * CT)
                dve.wait_ge(std_ready, c + 1)
                nc.vector.reciprocal(rstd[:, cols], std[:, cols]).then_inc(scale_ready, 1)
                dve.wait_ge(scale_ready, 2 * c + 1)
                nc.vector.scalar_tensor_tensor(shift[:, cols], mv[:, cols, 0], -1.0, rstd[:, cols], ALU.mult,
                                               ALU.mult).then_inc(scale_ready, 1)

            def normalise(g):
                if g >= XN:
                    dve.wait_ge(xT_ready, g - XN + 1)
                for k in range(GT - DVE_TILES[g], GT):
                    t = g * GT + k
                    last = nc.vector.tensor_scalar(xn[:, g % XN, k, :], xs[:, t, :], mv[:, t, 0:1],
                                                   rstd[:, t:t + 1], ALU.subtract, ALU.mult)
                last.then_inc(xn_dve, 1)

            for t in range(CT):
                moments(t)
            aggregate(0)
            for c in range(1, C):
                for k in range(CT):
                    moments(c * CT + k)
                    if k == 1:
                        scales(c - 1)
                        normalise(2 * c - 2)
                    if k == 4:
                        normalise(2 * c - 1)
                if c == 1:
                    dve.wait_ge(wa_mm, 1)
                    dve.wait_ge(consts_ready, 1)
                    nc.vector.tensor_copy(ww[:, S1:S1 + 1], ps[:, 7, 0:1])
                    nc.vector.tensor_scalar(ww[:, NS2:NS2 + 1], ps[:, 7, 1:2], -1.0, None, ALU.mult)
                    nc.vector.tensor_copy(ww[:, S2:S2 + 1], ps[:, 7, 1:2]).then_inc(ww_ready, 1)
                aggregate(c)

            def less(c):
                dve.wait_ge(xn_pool, 2 * c + 2)
                dve.wait_ge(xn_dve, 2 * c + 2)
                nc.vector.tensor_scalar(xs[:, c * CT:(c + 1) * CT, :], xs[:, c * CT:(c + 1) * CT, :], -1.0, None,
                                        ALU.add).then_inc(less_one, 1)

            scales(C - 1)
            normalise(G - 2)
            normalise(G - 1)
            less(0)
            less(1)
            for g in range(HA, G):
                if g == G - 1:
                    dve.wait_ge(yT_ready, G)
                    step(nc.vector.reduce_sum(ysum[:, G:G + 1], ysum[:, 0:G], AX.X))
                    nc.vector.tensor_copy(square[:, :], ysum[:, G:G + 1].to_broadcast([P, P])).then_inc(ysum_ready, 1)
                dve.wait_ge(h_mm, g + 1)
                v = ps[:, 2 + 2 * (g % 2):4 + 2 * (g % 2), :].rearrange("p b (k c) -> p (b k) c", k=2)
                nc.vector.tensor_copy(hs[:, g * GT:(g + 1) * GT, :], v[:, :, 0:HC]).then_inc(h_dve, 1)
                if g < HA + 2:
                    less(g - HA + 2)
            dve.wait_ge(h_act, HA)
            dve.wait_ge(h_dve, G - HA)
            nc.vector.tensor_reduce(st[:, 0:1], hs[:, :, S1:S1 + 2], AX.XY, ALU.max)
            nc.vector.reduce_max(st[:, 1:2], hs[:, :, S2], AX.X).then_inc(st_ready, 1)
            nc.vector.memset(hs[:, :, F:D], 1.0).then_inc(ones_col, 1)
            dve.wait_ge(hsum_mm, 1)
            nc.vector.tensor_copy(hsum[:, 0:F], ps[:, 0, 0:F]).then_inc(hsum_ready, 1)
            dve.wait_ge(st_turned, 1)
            nc.vector.reduce_max(top[:, :], ps[0:3, 6, 0:P], AX.X).then_inc(top_ready, 1)
            dve.wait_ge(mx_mm, 1)
            nc.vector.tensor_scalar(bias_cq[:, :], ps[:, 7, 0:1], SLOPE - 1.0, LOGTOP, ALU.mult, ALU.add)
            nc.vector.tensor_scalar(bias_v[:, :], ps[:, 7, 1:2], -1.0, None, ALU.mult).then_inc(bias_ready, 1)
            nc.vector.tensor_copy(mx[:, :], ps[:, 7, 0:3]).then_inc(mx_ready, 1)
            dve.wait_ge(cq_hi, 1)
            nc.vector.tensor_tensor(cqp16[:, :, :, 0], cqf[:, :, :], cqp16[:, :, :, 1], ALU.subtract).then_inc(cq_ready, 1)
            dve.wait_ge(mx_ready, 1)
            step(nc.vector.tensor_tensor(viol[:, 0:1], mx[:, 0:1], mx[:, 1:2], ALU.add))
            nc.vector.tensor_scalar(viol[:, 1:2], viol[:, 0:1], 1.0 - SLOPE, -WINDOW, ALU.mult, ALU.add)
            nc.vector.tensor_scalar(viol[:, 2:3], mx[:, 2:3], -NORM2_MAX, None, ALU.add)
            step(nc.vector.tensor_scalar(viol[:, 3:4], mx[:, 2:3], -1.0, NORM2_MIN, ALU.mult, ALU.add))
            step(nc.vector.reduce_max(viol[:, 0:1], viol[:, 1:4], AX.X))
            nc.vector.tensor_scalar(flag[:, :], viol[:, 0:1], 0.0, None, ALU.is_gt).then_inc(flag_ready, 1)
            for g in C_DVE:
                dve.wait_ge(c_turned, g + 1)
                nc.vector.tensor_copy(cp[:, g * GC:(g + 1) * GC], ps[:, g, :]).then_inc(c_dve, 1)

            def weights(s, jb, first):
                if first and jb == 0:
                    dve.wait_ge(c_dve, 1)
                    dve.wait_ge(c_act, 1)
                if jb < T - 1:
                    dve.wait_ge(mask_ready, s * T + (jb + 1))
                if jb >= WR:
                    dve.wait_ge(w_used, s * (T - 1) + (jb - WR + 1))
                elif not first and jb < WR - 1:
                    dve.wait_ge(w_used, (s - 1) * (T - 1) + (T - WR + jb + 1))
                elif not first:
                    dve.wait_ge(acc_done, s * 4)
                if jb == T - 1:
                    dve.wait_ge(mask_half, s + 1)
                    nc.vector.scalar_tensor_tensor(
                        w[:, jb % WR, 0:SH], cp[:, bass.ds(s * SC, SH)], cqp[:, jb, 1:2],
                        mask[:, jb % MR, 0:SH], ALU.max, ALU.min).then_inc(w_half, 1)
                    dve.wait_ge(mask_ready, s * T + T)
                    nc.vector.scalar_tensor_tensor(
                        w[:, jb % WR, SH:SC], cp[:, bass.ds(s * SC + SH, SH)], cqp[:, jb, 1:2],
                        mask[:, jb % MR, SH:SC], ALU.max, ALU.min).then_inc(w_ready, 1)
                else:
                    nc.vector.scalar_tensor_tensor(
                        w[:, jb % WR, :], cp[:, bass.ds(s * SC, SC)], cqp[:, jb, 1:2],
                        mask[:, jb % MR, :], ALU.max, ALU.min).then_inc(w_ready, 1)

            def add_low(s):
                for half in range(2):
                    dve.wait_ge(hi_copied, s * 2 + (half + 1))
                    b = slice(half * HB, (half + 1) * HB)
                    nc.vector.tensor_tensor(acc[:, b, :], acc[:, b, :], ps[:, b, D:2 * D], ALU.add).then_inc(acc_ready, 1)

            def blocks(s, first):
                for jb in range(T):
                    weights(s, jb, first)
                    if not first and jb == ADD_AT:
                        add_low(s - 1)
                    if not first and jb == ADD_AT + 1:
                        dve.wait_ge(acc_ready, s * 2)
                        nc.vector.reciprocal(rt[:, :], acc[:, :, F]).then_inc(rt_ready, 1)
                    if not first and jb == OUT_AT:
                        dve.wait_ge(exp_ready, s)
                        dve.wait_ge(relu_x, s)
                        nc.vector.scalar_tensor_tensor(res[:, :, :], en[:, :, :], 1.0, res[:, :, :], ALU.min,
                                                       ALU.add).then_inc(acc_free, 1)

            general = chosen(dve)
            with dve.If(general == 0):
                blocks(0, True)
                with dve.Fori(1, S) as s:
                    blocks(s, False)
                for k in range(4 + 1):
                    if k < 4:
                        b = slice(k * QB, (k + 1) * QB)
                        dve.wait_ge(hi_copied, (S - 1) * 2 + k + 1)
                        nc.vector.tensor_tensor(acc[:, b, :], acc[:, b, :], ps[:, b, D:2 * D],
                                                ALU.add).then_inc(acc_ready, 1)
                        dve.wait_ge(acc_ready, (S - 1) * 2 + k + 1)
                        nc.vector.reciprocal(rt[:, b], acc[:, b, F]).then_inc(rt_ready, 1)
                        dve.wait_ge(rt_ready, (S - 1) + k + 1)
                        if k == 0:
                            dve.wait_ge(out_done, 16 * (S - 1))
                        for i in range(k * QB, (k + 1) * QB):
                            last = nc.vector.tensor_scalar(res[:, i, :], acc[:, i, 0:F], rt[:, i:i + 1], 0.0,
                                                           ALU.mult, ALU.max)
                        last.then_inc(last_relu, 1)
                    if k >= 1:
                        b = slice((k - 1) * QB, k * QB)
                        dve.wait_ge(exp_ready, S - 1 + k)
                        dve.wait_ge(relu_x, S - 1 + k)
                        nc.vector.scalar_tensor_tensor(res[:, b, :], en[:, b, :], 1.0, res[:, b, :], ALU.min,
                                                       ALU.add).then_inc(last_res, 1)
            with dve.If(general == 1):
                dve.wait_ge(less_one, C)
                dve.wait_ge(g_ready, 1)
                dve.wait_ge(c_act, len(C_ACT))
                with dve.Fori(0, T) as t:
                    nc.vector.tensor_copy(square[:, :], hs[:, bass.ds(t, 1), S2].to_broadcast([P, P])).then_inc(gen_col, 1)
                    dve.wait_ge(gen_row, t + 1)
                    nc.vector.tensor_copy(s2_bc_t[:, bass.ds(t, 1), :],
                                          ps[:, 0, 0:P].unsqueeze(1)).then_inc(gen_s2, 1)
                    dve.wait_ge(gen_s2, t + 1)
                STEPS = 7

                def row_tile(t, first):
                    done = [0]

                    def gstep(ins):
                        done[0] += 1
                        ins.then_inc(gen_step, 1)
                        dve.wait_ge(gen_step, t * STEPS + done[0])

                    dve.wait_ge(gen_adj, 16 * (t + 1))
                    nc.vector.tensor_scalar(penalty, row_adj, 0.0, NEG, ALU.is_le, ALU.mult)
                    gstep(nc.vector.tensor_scalar(scores, s2_bc, hs[:, bass.ds(t, 1), S1], None, ALU.add))
                    gstep(nc.vector.scalar_tensor_tensor(scores, scores, SLOPE, scores, ALU.mult, ALU.max))
                    gstep(nc.vector.tensor_tensor(scores, scores, penalty, ALU.add))
                    gstep(nc.vector.reduce_max(g_cols[:, 2:3], scores, AX.X))
                    nc.vector.tensor_scalar(neg_max, g_cols[:, 2:3], -1.0, None, ALU.mult).then_inc(gen_scores, 1)
                    dve.wait_ge(gen_probs, t + 1)
                    gstep(nc.vector.reciprocal(g_cols[:, 3:4], den))
                    dve.wait_ge(gen_num, t + 1)
                    if not first:
                        dve.wait_ge(gen_out, 16 * t)
                    gstep(nc.vector.tensor_scalar(g_hp, ps[:, 1, 0:F], g_cols[:, 3:4], None, ALU.mult))
                    nc.vector.tensor_scalar(g_en, g_hp, 0.0, None, ALU.min).then_inc(gen_min, 1)
                    dve.wait_ge(gen_exp, t + 1)
                    gstep(nc.vector.scalar_tensor_tensor(g_hp, g_hp, 0.0, g_en, ALU.max, ALU.add))
                    nc.vector.tensor_tensor(g_res.unsqueeze(1), g_hp.unsqueeze(1), xs[:, bass.ds(t, 1), :],
                                            ALU.add).then_inc(gen_res, 1)

                row_tile(0, True)
                with dve.Fori(1, T) as t:
                    row_tile(t, False)

    return nc

def kernel(x, adj, L0_gnn_W, L0_gnn_a):
    import numpy as _np
    import concourse.bacc as _bacc
    from concourse import mybir as _mybir
    from concourse.bass_utils import run_bass_kernel_spmd as _run

    nc = _bacc.Bacc("TRN2", target_bir_lowering=False, num_devices=1)
    x, adj, W, a = (_np.asarray(v) for v in (x, adj, L0_gnn_W, L0_gnn_a))
    blocks = adj.reshape(128, 4, 8, 128, 32).transpose(1, 4, 3, 2, 0).reshape(128, 128, 1024)
    arrays = {
        "x": _np.ascontiguousarray(x),
        "adj": _np.ascontiguousarray(adj),
        "adjT": _np.ascontiguousarray(blocks),
        "W": _np.ascontiguousarray(W),
        "wT": _np.ascontiguousarray(W.T),
        "a": _np.ascontiguousarray(a.reshape(2, 128).T),
    }
    args = [nc.dram_tensor(f"in_{n}", v.shape, _mybir.dt.from_np(v.dtype), kind="ExternalInput").ap()
            for n, v in arrays.items()]
    args.append(nc.dram_tensor("out", x.shape, _mybir.dt.float32, kind="ExternalOutput").ap())
    gat_kernel(nc, *args)
    r = _run(nc, [{f"in_{n}": v for n, v in arrays.items()}], core_ids=[0])
    return r.results[0]["out"]
```
